# Optimizing a Trainium2 kernel written in Bass

```python
import numpy as np
import jax
import jax.numpy as jnp

def _softmax(x, axis=-1):
    return jax.nn.softmax(x, axis=axis)

def _gelu(x):
    return jax.nn.gelu(x, approximate=True)

def _silu(x):
    return jax.nn.silu(x)

def _sigmoid(x):
    return jax.nn.sigmoid(x)

def _layernorm(x, axis=-1, eps=1e-05):
    m = jnp.mean(x, axis=axis, keepdims=True)
    v = jnp.var(x, axis=axis, keepdims=True)
    return (x - m) / jnp.sqrt(v + eps)

def _scatter_add(tgt, idx, src, axis=0):
    return tgt.at[idx].add(src)

def _segment_sum(src, seg, n):
    return jax.ops.segment_sum(src, seg, n)
kernel_name = 'mk_adj_seq_d1_adj_r2_f25e41'

def setup_inputs(seed: int=0):
    np.random.seed(seed)
    _w = jnp.asarray

    def _rec_inputs():
        import jax
        import jax.numpy as jnp
        _gk = jax.random.key(seed)
        x = -0.0005207 + 1.001 * jax.random.normal(jax.random.fold_in(_gk, 1), (8192, 256), jnp.float32)
        _w = (1.0 + jnp.arange(8192, dtype=jnp.float32)) ** (-0.5)
        _w = _w / _w.mean()
        _pij = jnp.clip(0.000244141 * _w[:, None] * _w[None, :], 0.0, 1.0)
        _a = jax.random.uniform(jax.random.fold_in(_gk, 2), (8192, 8192)) < _pij
        adj = _a.astype(jnp.int32)
        return (x, adj)
    x, adj = _rec_inputs()

    def _L0_gnn_setup():
        import jax, jax.numpy as jnp
        import numpy as np
        N, DIM = (2048, 256)
        F_OUT = DIM // 8
        HID = int(DIM * 2.0)
        ALPHA = 0.2
        MASK_VAL = -9000000000000000.0

        def _layernorm(x, g, b, eps=1e-05):
            mu = x.mean(-1, keepdims=True)
            var = ((x - mu) ** 2).mean(-1, keepdims=True)
            return (x - mu) * jax.lax.rsqrt(var + eps) * g + b
        key = jax.random.key(seed)
        ks = jax.random.split(key, 8)
        x = jax.random.normal(ks[0], (N, DIM), jnp.float32)
        adj = jax.random.randint(ks[1], (N, N), 0, 2, jnp.int32)
        W = jax.random.normal(ks[2], (DIM, F_OUT), jnp.float32) * 0.1
        a = jax.random.normal(ks[3], (2 * F_OUT, 1), jnp.float32) * 0.1
        fc_w = jax.random.normal(ks[4], (DIM, F_OUT), jnp.float32) * 0.1
        fc_b = jnp.zeros((DIM,), jnp.float32)
        ln1_g = jnp.ones((DIM,), jnp.float32)
        ln1_b = jnp.zeros((DIM,), jnp.float32)
        ln2_g = jnp.ones((DIM,), jnp.float32)
        ln2_b = jnp.zeros((DIM,), jnp.float32)
        fc1_w = jax.random.normal(ks[5], (HID, DIM), jnp.float32) * 0.05
        fc1_b = jnp.zeros((HID,), jnp.float32)
        fc2_w = jax.random.normal(ks[6], (DIM, HID), jnp.float32) * 0.05
        fc2_b = jnp.zeros((DIM,), jnp.float32)
        return dict(x=x, adj=adj, W=W, a=a, fc_w=fc_w, fc_b=fc_b, ln1_g=ln1_g, ln1_b=ln1_b, ln2_g=ln2_g, ln2_b=ln2_b, fc1_w=fc1_w, fc1_b=fc1_b, fc2_w=fc2_w, fc2_b=fc2_b)
    _L0_gnn_all = _L0_gnn_setup()
    _L0_gnn_in = {k: v for k, v in _L0_gnn_all.items() if k in ('W', 'a', 'fc_w', 'fc_b', 'ln1_g', 'ln1_b', 'ln2_g', 'ln2_b', 'fc1_w', 'fc1_b', 'fc2_w', 'fc2_b')}
    del _L0_gnn_all
    return {'x': x, 'adj': adj, 'L0_gnn_W': _L0_gnn_in['W'], 'L0_gnn_a': _L0_gnn_in['a'], 'L0_gnn_fc_w': _L0_gnn_in['fc_w'], 'L0_gnn_fc_b': _L0_gnn_in['fc_b'], 'L0_gnn_ln1_g': _L0_gnn_in['ln1_g'], 'L0_gnn_ln1_b': _L0_gnn_in['ln1_b'], 'L0_gnn_ln2_g': _L0_gnn_in['ln2_g'], 'L0_gnn_ln2_b': _L0_gnn_in['ln2_b'], 'L0_gnn_fc1_w': _L0_gnn_in['fc1_w'], 'L0_gnn_fc1_b': _L0_gnn_in['fc1_b'], 'L0_gnn_fc2_w': _L0_gnn_in['fc2_w'], 'L0_gnn_fc2_b': _L0_gnn_in['fc2_b']}

def reference(x, adj, L0_gnn_W, L0_gnn_a, L0_gnn_fc_w, L0_gnn_fc_b, L0_gnn_ln1_g, L0_gnn_ln1_b, L0_gnn_ln2_g, L0_gnn_ln2_b, L0_gnn_fc1_w, L0_gnn_fc1_b, L0_gnn_fc2_w, L0_gnn_fc2_b):
    import jax
    import jax.numpy as jnp

    def _L0_gnn_ref(x, adj, W, a, fc_w, fc_b, ln1_g, ln1_b, ln2_g, ln2_b, fc1_w, fc1_b, fc2_w, fc2_b):
        import jax, jax.numpy as jnp
        import numpy as np
        N, DIM = (2048, 256)
        F_OUT = DIM // 8
        HID = int(DIM * 2.0)
        ALPHA = 0.2
        MASK_VAL = -9000000000000000.0

        def _layernorm(x, g, b, eps=1e-05):
            mu = x.mean(-1, keepdims=True)
            var = ((x - mu) ** 2).mean(-1, keepdims=True)
            return (x - mu) * jax.lax.rsqrt(var + eps) * g + b
        h = _layernorm(x, ln1_g, ln1_b)
        Wh = h @ W
        f_src = Wh @ a[:F_OUT, 0]
        f_dst = Wh @ a[F_OUT:, 0]
        e = f_src[:, None] + f_dst[None, :]
        e = jnp.where(e >= 0, e, ALPHA * e)
        att = jax.nn.softmax(jnp.where(adj > 0, e, MASK_VAL), axis=1)
        h_prime = att @ Wh
        attn_out = h_prime @ fc_w.T + fc_b
        x = x + attn_out
        h2 = _layernorm(x, ln2_g, ln2_b)
        m = jax.nn.gelu(h2 @ fc1_w.T + fc1_b, approximate=False)
        m = m @ fc2_w.T + fc2_b
        return x + m
    x = _L0_gnn_ref(x, adj, L0_gnn_W, L0_gnn_a, L0_gnn_fc_w, L0_gnn_fc_b, L0_gnn_ln1_g, L0_gnn_ln1_b, L0_gnn_ln2_g, L0_gnn_ln2_b, L0_gnn_fc1_w, L0_gnn_fc1_b, L0_gnn_fc2_w, L0_gnn_fc2_b)
    return x

_drawn_inputs = setup_inputs


def setup_inputs(seed=0):
    import zlib

    import numpy as np

    out = dict(_drawn_inputs(seed))
    spreads = {'L0_gnn_fc_b': (0.0, 0.1),
     'L0_gnn_ln1_g': (1.0, 0.2),
     'L0_gnn_ln1_b': (0.0, 0.1),
     'L0_gnn_ln2_g': (1.0, 0.2),
     'L0_gnn_ln2_b': (0.0, 0.1),
     'L0_gnn_fc1_b': (0.0, 0.1),
     'L0_gnn_fc2_b': (0.0, 0.1)}
    factors = {}
    for name, (base, spread) in spreads.items():
        noise = np.random.default_rng([zlib.crc32(name.encode()), seed]).standard_normal(out[name].shape)
        drawn = base * np.exp(spread * noise) if base else spread * noise
        out[name] = jnp.asarray(drawn.astype(out[name].dtype))
    for name, factor in factors.items():
        out[name] = (out[name] * factor).astype(out[name].dtype)
    return out
```

```python
from contextlib import ExitStack

import concourse.bass as bass
from concourse import mybir

F32 = mybir.dt.float32
BF16 = mybir.dt.bfloat16
ALU = mybir.AluOpType
ACT = mybir.ActivationFunctionType
AX_X = mybir.AxisListType.X
RMAX = bass.bass_isa.ReduceOp.max

P = 128
ALPHA = 0.2
EPS = 1e-5
PARTS = 3
STEEP = 2.0 ** 40


def build_gat(nc, x, adj, w, w_t, a_pair, fc_t, fc_b, ln1_gb, ln2_gb, fc1_t, fc1_b, fc2_t, fc2_b, out):
    N, DIM = x.shape
    F = w.shape[1]
    FO = F + 1
    HID = fc1_t.shape[1]
    KC = DIM // P
    HC = HID // P
    JB = N // P
    ROWS = 512
    RB = ROWS // P
    GROUPS = N // ROWS
    UNIT = 4
    UNITS = JB // UNIT
    CHUNKS = UNITS // 2
    CCOLS = N // CHUNKS
    RING = 4
    AHEAD = RING - 1
    W3 = PARTS * FO
    CONSTS = 6
    CONSTS_ALL = CONSTS + PARTS + 2
    NODE_STEPS = 7
    ATT_STEPS = 8
    BAT = 16

    x_v = x.rearrange("(n p) d -> p n d", p=P)
    adj_v = adj.rearrange("(n p) j -> p n j", p=P)
    out_v = out.rearrange("(n p) d -> p n d", p=P)

    with ExitStack() as ctx:
        def sb(name, shape, dt=F32):
            return ctx.enter_context(nc.sbuf_tensor(name, shape, dt))

        def pb(name, shape, dt=F32):
            return ctx.enter_context(nc.psum_tensor(name, shape, dt))

        def sem(name):
            return ctx.enter_context(nc.semaphore(name))

        w_aug = sb("w_aug", [P, KC, F + 2])
        w_src = sb("w_src", [P, KC, P])
        w_tr = sb("w_tr", [F, DIM])
        a_sd = sb("a_sd", [F, 2])
        fc_sb = sb("fc_sb", [F, DIM])
        fcb_row = sb("fcb_row", [P, DIM])
        fc2b_row = sb("fc2b_row", [P, DIM])
        ln1 = sb("ln1", [P, 2, KC])
        ln2 = sb("ln2", [P, 2, KC])
        fc1_sb = sb("fc1_sb", [P, KC, HID])
        fc1b = sb("fc1b", [P, HC])
        fc2_sb = sb("fc2_sb", [P, HC, DIM])
        ident = sb("ident", [P, P])
        identb = sb("identb", [P, P], BF16)
        ones_n = sb("ones_n", [P, P])
        fold3 = sb("fold3", [W3, FO])
        minus_half = sb("minus_half", [P, RB])
        eps = sb("eps", [P, RB])
        scratch = sb("scratch", [P, 1])

        wh = sb("wh", [P, JB, FO])
        sd = sb("sd", [P, 2, JB])
        s_rows = sb("s_rows", [P, N])
        s_now = sb("s_now", [P, ROWS])
        steep_d = sb("steep_d", [P, JB])
        edge = sb("edge", [P, 2])
        edge_all = sb("edge_all", [P, 2])
        neg_d = sb("neg_d", [P, JB])
        d_shift = sb("d_shift", [P, JB])
        s_top = sb("s_top", [P, JB])
        s_guard = sb("s_guard", [P, JB])
        row_args = sb("row_args", [P, 2, JB])
        row_scale = sb("row_scale", [P, 2, JB])
        col_scale = sb("col_scale", [P, 2, JB])
        wh_sum = sb("wh_sum", [P, F])
        mean_row = sb("mean_row", [P, F])
        vals = [sb(f"vals{k}", [P, JB, W3], BF16) for k in range(2)]
        cut = [sb(f"cut{k}", [P, BAT, FO]) for k in range(2)]

        masks = [sb(f"masks{k}", [P, RB, CCOLS], BF16) for k in range(RING)]
        above = [sb(f"above{k}", [P, UNIT, ROWS], BF16) for k in range(2)]
        pos = [sb(f"pos{k}", [P, UNIT, ROWS], BF16) for k in range(2)]
        neg = [sb(f"neg{k}", [P, UNIT, ROWS], BF16) for k in range(2)]

        sums = sb("sums", [W3, 2, ROWS])
        scaled = [sb(f"scaled{k}", [P, RB, FO]) for k in range(2)]
        total = sb("total", [P, RB, FO])
        lonely = sb("lonely", [P, RB])
        lonely_mean = sb("lonely_mean", [P, RB, F])
        denom = sb("denom", [P, RB])
        inv_denom = sb("inv_denom", [P, RB])
        numer = sb("numer", [P, RB, F])
        att = sb("att", [P, RB, F])
        att_t = sb("att_t", [F, ROWS])
        x_in = [sb(f"x_in{k}", [P, RB, DIM]) for k in range(2)]
        x_fcb = x_in[1]
        x_mid = sb("x_mid", [P, RB, DIM])
        x_fc2b = sb("x_fc2b", [P, RB, DIM])
        h_n = sb("h_n", [P, RB, DIM])
        h_t = sb("h_t", [P, KC, ROWS])
        act_t = sb("act_t", [P, HC, ROWS])
        y_out = sb("y_out", [P, RB, DIM])
        stats = [sb(f"stats{k}", [P, RB, 6]) for k in range(2)]
        mean_var = [sb(f"mean_var{k}", [P, RB, 2]) for k in range(2)]
        var_eps = sb("var_eps", [P, RB])
        rstd = [sb(f"rstd{k}", [P, RB]) for k in range(2)]

        flipped = [pb(f"flipped{k}", [P, UNIT, ROWS], BF16) for k in range(2)]
        acc = [pb(f"acc{k}", [P, ROWS]) for k in range(2)]
        tail = [pb(f"tail{k}", [P, ROWS]) for k in range(2)]

        w_landed = sem("w_landed")
        gb_landed = sem("gb_landed")
        tail_w_landed = sem("tail_w_landed")
        x_landed = [sem(f"x_landed{k}") for k in range(2)]
        consts = sem("consts")
        wa_ready = sem("wa_ready")
        wa_saved = sem("wa_saved")
        stat_step = sem("stat_step")
        stats_done = sem("stats_done")
        rstd_step = sem("rstd_step")
        rstd_done = sem("rstd_done")
        normed = sem("normed")
        h_flipped = sem("h_flipped")
        h_t_done = sem("h_t_done")
        projected = sem("projected")
        s_saved = sem("s_saved")
        wh_saved = sem("wh_saved")
        node_step = sem("node_step")
        edges_local = sem("edges_local")
        edges_done = sem("edges_done")
        scales_ready = sem("scales_ready")
        wh_summed = sem("wh_summed")
        mean_ready = sem("mean_ready")
        mean_saved = sem("mean_saved")
        cut_step = sem("cut_step")
        vals_ready = sem("vals_ready")

        adj_landed = [sem(f"adj_landed{k}") for k in range(RING)]
        mask_ready = sem("mask_ready")
        chunk_flipped = sem("chunk_flipped")
        unit_flipped = sem("unit_flipped")
        rows_taken = sem("rows_taken")
        above_ready = sem("above_ready")
        pos_ready = sem("pos_ready")
        neg_ready = sem("neg_ready")
        unit_added = sem("unit_added")
        sums_saved = sem("sums_saved")
        folded = sem("folded")
        att_step = sem("att_step")
        att_flipped = sem("att_flipped")
        att_t_ready = sem("att_t_ready")
        proj_ready = sem("proj_ready")
        x_fcb_ready = sem("x_fcb_ready")
        x_mid_ready = sem("x_mid_ready")
        stats2_step = sem("stats2_step")
        stats2_done = sem("stats2_done")
        rstd2_step = sem("rstd2_step")
        rstd2_done = sem("rstd2_done")
        x_fc2b_ready = sem("x_fc2b_ready")
        normed2 = sem("normed2")
        h2_flipped = sem("h2_flipped")
        h2_t_done = sem("h2_t_done")
        fc1_ready = sem("fc1_ready")
        gelu_done = sem("gelu_done")
        fc2_ready = sem("fc2_ready")
        y_ready = sem("y_ready")
        y_stored = sem("y_stored")
        x2_landed = sem("x2_landed")

        def over_groups(eng, body):
            body(0, first=True)
            with eng.Fori(1, GROUPS - 1) as g:
                body(g)
            body(GROUPS - 1, last=True)

        def over_pairs(eng, body):
            body(0, first=True)
            with eng.Fori(1, GROUPS // 2 - 1) as i:
                body(i)
            body(GROUPS // 2 - 1, last=True)

        block = ctx.enter_context(nc.Block())

        @block.sync
        def _(sp):
            def load_x(k, n):
                return sp.dma_start(x_in[k][:], x_v[:, bass.ds(n * RB, RB), :])

            load_x(0, 0).then_inc(x_landed[0], 16)
            sp.dma_start(w_aug[:, :, 0:F], w.rearrange("(c p) f -> p c f", p=P)).then_inc(w_landed, 16)
            sp.dma_start(w_tr[:], w_t).then_inc(w_landed, 16)
            sp.dma_start(a_sd[:], a_pair).then_inc(w_landed, 16)
            load_x(1, 1).then_inc(x_landed[1], 16)
            sp.dma_start(ln1[:], ln1_gb).then_inc(gb_landed, 16)
            sp.dma_start(ln2[:], ln2_gb).then_inc(gb_landed, 16)
            sp.dma_start(fc1b[:], fc1_b).then_inc(gb_landed, 16)
            sp.dma_start(fc_sb[:], fc_t).then_inc(tail_w_landed, 16)
            sp.dma_start(fc1_sb[:], fc1_t.rearrange("(c p) h -> p c h", p=P)).then_inc(tail_w_landed, 16)
            sp.dma_start(fc2_sb[:], fc2_t.rearrange("(c p) d -> p c d", p=P)).then_inc(tail_w_landed, 16)
            sp.dma_start(fcb_row[:], fc_b.to_broadcast([P, DIM])).then_inc(tail_w_landed, 16)
            sp.dma_start(fc2b_row[:], fc2_b.to_broadcast([P, DIM])).then_inc(tail_w_landed, 16)

            with sp.Fori(1, GROUPS // 2) as i:
                for k in range(2):
                    sp.wait_ge(normed, i * 2 + k - 1)
                    load_x(k, i * 2 + k).then_inc(x_landed[k], 16)

            def store(q, part):
                half = RB // 2
                sp.wait_ge(y_ready, q * 2 + part + 1)
                sp.dma_start(out_v[:, bass.ds(q * RB + part * half, half), :],
                             y_out[:, part * half:(part + 1) * half, :]).then_inc(y_stored, 16)

            def finish(q, first=False):
                if not first:
                    sp.wait_ge(x_fcb_ready, q)
                    sp.wait_ge(y_stored, q * 2 * 16)
                load_x(0, q).then_inc(x2_landed, 16)
                store(q, 0)
                store(q, 1)

            sp.wait_ge(normed, GROUPS)
            finish(0, first=True)
            with sp.Fori(1, GROUPS) as q:
                finish(q)
            sp.wait_ge(y_stored, 16 * 2 * GROUPS)

        @block.gpsimd
        def _(pool):
            def load_chunk(g, c):
                pool.dma_start(masks[c % RING][:], adj_v[:, bass.ds(g * RB, RB), c * CCOLS:(c + 1) * CCOLS])\
                    .then_inc(adj_landed[c % RING], 16)

            for c in range(AHEAD):
                load_chunk(0, c)

            nc.gpsimd.memset(ident[:], 0.0).then_inc(consts, 1)
            nc.gpsimd.memset(fold3[:], 0.0).then_inc(consts, 1)
            nc.gpsimd.memset(minus_half[:], -0.5).then_inc(consts, 1)
            nc.gpsimd.memset(eps[:], EPS).then_inc(consts, 1)
            nc.gpsimd.memset(wh[:], 1.0).then_inc(consts, 1)
            nc.gpsimd.memset(ones_n[:], 1.0 / N).then_inc(consts, 1)
            pool.wait_ge(consts, CONSTS)
            nc.gpsimd.affine_select(out=ident[:], in_=ident[:], compare_op=ALU.not_equal, fill=1.0,
                                    base=0, pattern=[[-1, P]], channel_multiplier=1).then_inc(consts, 1)
            for part in range(PARTS):
                nc.gpsimd.affine_select(out=fold3[:], in_=fold3[:], compare_op=ALU.not_equal, fill=1.0,
                                        base=-part * FO, pattern=[[-1, FO]], channel_multiplier=1)\
                    .then_inc(consts, 1)
                pool.wait_ge(consts, CONSTS + 2 + part)
            nc.gpsimd.tensor_copy(identb[:], ident[:]).then_inc(consts, 1)

            def inverse_deviation(step, base, mv, to, done):
                nc.gpsimd.tensor_tensor(var_eps[:], mv[:, :, 1], eps[:], ALU.add).then_inc(step, 1)
                pool.wait_ge(step, base + 1)
                nc.gpsimd.tensor_tensor(to[:], var_eps[:], minus_half[:], ALU.pow).then_inc(done, 1)
                pool.wait_ge(done, base + 1)

            with pool.Fori(0, GROUPS // 2) as i:
                for k in range(2):
                    pool.wait_ge(stats_done, i * 2 + k + 1)
                    inverse_deviation(rstd_step, i * 2 + k, mean_var[k], rstd[k], rstd_done)

            pool.wait_ge(edges_local, 2)
            nc.gpsimd.partition_all_reduce(edge_all[:], edge[:], P, RMAX).then_inc(edges_done, 1)

            pool.wait_ge(tail_w_landed, 5 * 16)

            def body(g, first=False, last=False):
                q = g - 1
                for c in range(CHUNKS):
                    if not (last and c + AHEAD >= CHUNKS):
                        if not (first and c == 0):
                            pool.wait_ge(chunk_flipped, g * CHUNKS + c)
                        ahead = c + AHEAD
                        load_chunk(g + ahead // CHUNKS, ahead % CHUNKS)
                    if not first:
                        finish_rows(q, c)

            def finish_rows(q, c):
                if c == 0:
                    pool.wait_ge(x2_landed, 16 * (q + 1))
                    nc.gpsimd.tensor_tensor(x_fcb[:], x_in[0][:],
                                            fcb_row[:].unsqueeze(1).to_broadcast([P, RB, DIM]),
                                            ALU.add).then_inc(x_fcb_ready, 1)
                if c == 2:
                    pool.wait_ge(stats2_done, q + 1)
                    inverse_deviation(rstd2_step, q, mean_var[0], rstd[0], rstd2_done)
                    pool.wait_ge(x_mid_ready, q + 1)
                    nc.gpsimd.tensor_tensor(x_fc2b[:], x_mid[:],
                                            fc2b_row[:].unsqueeze(1).to_broadcast([P, RB, DIM]),
                                            ALU.add).then_inc(x_fc2b_ready, 1)

            over_groups(pool, body)
            for c in range(CHUNKS):
                finish_rows(GROUPS - 1, c)

        def affine_flip(act, gb, ready):
            for c in range(KC):
                last = nc.scalar.activation(h_t[:, c, :], tail[c][:], ACT.Identity,
                                            bias=gb[:, 1, c:c + 1], scale=gb[:, 0, c:c + 1])
            last.then_inc(ready, 1)

        @block.scalar
        def _(act):
            act.wait_ge(gb_landed, 3 * 16)
            act.wait_ge(wa_ready, 1)
            for c in range(KC):
                nc.scalar.activation(w_aug[:, c, F:F + 2], tail[0][:, 2 * c:2 * c + 2], ACT.Copy)
                last = nc.scalar.activation(w_src[:, c, :], tail[1][:, c * P:(c + 1) * P], ACT.Copy)
            last.then_inc(wa_saved, 1)

            with act.Fori(0, GROUPS) as t:
                act.wait_ge(h_flipped, t + 1)
                affine_flip(act, ln1, h_t_done)
                act.wait_ge(projected, t + 1)
                nc.scalar.activation(s_rows[:, bass.ds(t * ROWS, ROWS)], acc[1][:], ACT.Copy)\
                    .then_inc(s_saved, 1)

            act.wait_ge(node_step, NODE_STEPS)
            nc.scalar.activation(col_scale[:, 0, :], d_shift[:], ACT.Exp)
            nc.scalar.activation(col_scale[:, 1, :], d_shift[:], ACT.Exp, scale=ALPHA)
            nc.scalar.activation(row_scale[:], row_args[:], ACT.Exp).then_inc(scales_ready, 1)

            def mark(g, u):
                for j in range(UNIT):
                    jb = u * UNIT + j
                    last = nc.scalar.activation(above[u % 2][:, j, :], s_now[:],
                                                ACT.Relu, bias=steep_d[:, jb:jb + 1])
                last.then_inc(above_ready, 1)

            def finish_rows(q, u):
                if u == 0:
                    act.wait_ge(unit_added, (q + 1) * UNITS)
                    for k in range(2):
                        last = nc.scalar.activation(sums[:, k, :], acc[k][0:W3, :], ACT.Copy)
                    last.then_inc(sums_saved, 1)
                if u == 3:
                    act.wait_ge(att_flipped, q + 1)
                    nc.scalar.activation(att_t[:], tail[1][0:F, :], ACT.Copy).then_inc(att_t_ready, 1)
                if u == 7:
                    act.wait_ge(h2_flipped, q + 1)
                    affine_flip(act, ln2, h2_t_done)
                if 8 <= u < 8 + HC:
                    m = u - 8
                    act.wait_ge(fc1_ready, q * HC + m + 1)
                    nc.scalar.activation(act_t[:, m, :], tail[m % 2][:], ACT.Gelu,
                                         bias=fc1b[:, m:m + 1]).then_inc(gelu_done, 1)

            def body(g, first=False, last=False):
                for u in range(UNITS):
                    if not (last and u == UNITS - 1):
                        if u == UNITS - 1:
                            act.wait_ge(rows_taken, g + 2)
                        if not (first and u == 0):
                            act.wait_ge(pos_ready, g * UNITS + u)
                        nxt = u + 1
                        mark(g + nxt // UNITS, nxt % UNITS)
                    if not first:
                        finish_rows(g - 1, u)

            act.wait_ge(rows_taken, 1)
            mark(0, 0)
            over_groups(act, body)
            for u in range(UNITS):
                finish_rows(GROUPS - 1, u)

        @block.tensor
        def _(pe):
            pe.wait_ge(w_landed, 3 * 16)
            for c in range(KC):
                nc.tensor.matmul(tail[0][:, 2 * c:2 * c + 2], w_tr[:, c * P:(c + 1) * P], a_sd[:],
                                 start=True, stop=True)
                last = nc.tensor.matmul(tail[1][:, c * P:(c + 1) * P], w_tr[:, c * P:(c + 1) * P],
                                        a_sd[:, 0:1].to_broadcast([F, P]), start=True, stop=True)
            last.then_inc(wa_ready, 1)
            pe.wait_ge(consts, CONSTS_ALL)
            pe.wait_ge(wa_saved, 1)

            def flip_rows(done):
                for c in range(KC):
                    for r in range(RB):
                        last = nc.tensor.transpose(tail[c][:, r * P:(r + 1) * P],
                                                   h_n[:, r, c * P:(c + 1) * P], ident[:])
                last.then_inc(done, 1)

            def project(t, first=False):
                pe.wait_ge(normed, t + 1)
                if not first:
                    pe.wait_ge(h_t_done, t)
                flip_rows(h_flipped)
                pe.wait_ge(h_t_done, t + 1)
                if not first:
                    pe.wait_ge(wh_saved, t)
                    pe.wait_ge(s_saved, t)
                for r in range(RB):
                    for c in range(KC):
                        nc.tensor.matmul(acc[0][:, r * (F + 2):(r + 1) * (F + 2)],
                                         h_t[:, c, r * P:(r + 1) * P], w_aug[:, c, :],
                                         start=(c == 0), stop=(c == KC - 1))
                for c in range(KC):
                    last = nc.tensor.matmul(acc[1][:], w_src[:, c, :], h_t[:, c, :],
                                            start=(c == 0), stop=(c == KC - 1))
                last.then_inc(projected, 1)

            project(0, first=True)
            with pe.Fori(1, GROUPS) as t:
                project(t)

            pe.wait_ge(wh_summed, 1)
            pe.wait_ge(h_t_done, GROUPS)
            nc.tensor.matmul(tail[0][:, 0:F], ones_n[:], wh_sum[:], start=True, stop=True).then_inc(mean_ready, 1)
            pe.wait_ge(mean_saved, 1)

            def flip(g, u):
                c = u // 2
                if u % 2 == 0:
                    pe.wait_ge(mask_ready, g * CHUNKS + c + 1)
                for j in range(UNIT):
                    col = (u % 2 * UNIT + j) * P
                    for r in range(RB):
                        last = nc.tensor.transpose(flipped[u % 2][:, j, r * P:(r + 1) * P],
                                                   masks[c % RING][:, r, col:col + P], identb[:])
                last.then_inc(unit_flipped, 1)
                if u % 2:
                    pe.wait_ge(unit_flipped, g * UNITS + u + 1)
                    pe.sem_inc(chunk_flipped, 1)

            def add(g, u):
                for k, side, ready in ((0, pos, pos_ready), (1, neg, neg_ready)):
                    pe.wait_ge(ready, g * UNITS + u + 1)
                    for j in range(UNIT):
                        jb = u * UNIT + j
                        last = nc.tensor.matmul(acc[k][0:W3, :], vals[k][:, jb, :], side[u % 2][:, j, :],
                                                start=(jb == 0), stop=(jb == JB - 1))
                last.then_inc(unit_added, 1)

            def finish_rows(q, u):
                if u == 1:
                    pe.wait_ge(sums_saved, q + 1)
                    for r in range(RB):
                        for k in range(2):
                            last = nc.tensor.matmul(tail[0][:, (2 * r + k) * FO:(2 * r + k + 1) * FO],
                                                    sums[:, k, r * P:(r + 1) * P], fold3[:],
                                                    start=True, stop=True)
                    last.then_inc(folded, 1)
                if u == 3:
                    pe.wait_ge(att_step, (q + 1) * ATT_STEPS)
                    for r in range(RB):
                        last = nc.tensor.transpose(tail[1][0:F, r * P:(r + 1) * P], att[:, r, :], ident[:])
                    last.then_inc(att_flipped, 1)
                if u == 4:
                    pe.wait_ge(att_t_ready, q + 1)
                    for r in range(RB):
                        last = nc.tensor.matmul(tail[r // 2][:, r % 2 * DIM:(r % 2 + 1) * DIM],
                                                att_t[:, r * P:(r + 1) * P], fc_sb[:], start=True, stop=True)
                    last.then_inc(proj_ready, 1)
                if u == 7:
                    pe.wait_ge(normed2, q + 1)
                    flip_rows(h2_flipped)
                if 8 <= u < 8 + HC:
                    m = u - 8
                    pe.wait_ge(h2_t_done, q + 1)
                    if m >= 2:
                        pe.wait_ge(gelu_done, q * HC + m - 1)
                    for c in range(KC):
                        last = nc.tensor.matmul(tail[m % 2][:], fc1_sb[:, c, m * P:(m + 1) * P], h_t[:, c, :],
                                                start=(c == 0), stop=(c == KC - 1))
                    last.then_inc(fc1_ready, 1)
                if 12 <= u < 15:
                    pe.wait_ge(gelu_done, (q + 1) * HC)
                    for r in ((0,), (1,), (2, 3))[u - 12]:
                        for m in range(HC):
                            last = nc.tensor.matmul(tail[r // 2][:, r % 2 * DIM:(r % 2 + 1) * DIM],
                                                    act_t[:, m, r * P:(r + 1) * P], fc2_sb[:, m, :],
                                                    start=(m == 0), stop=(m == HC - 1))
                    if u > 12:
                        last.then_inc(fc2_ready, 1)

            def body(g, first=False, last=False):
                for u in range(UNITS):
                    if not (first and u < 2):
                        pe.wait_ge(neg_ready, g * UNITS + u - 1)
                    flip(g, u)
                    if u > 0:
                        if u == 1 and not first:
                            pe.wait_ge(sums_saved, g)
                        if first and (u - 1) % (BAT // UNIT) == 0:
                            pe.wait_ge(vals_ready, (u - 1) // (BAT // UNIT) + 1)
                        add(g, u - 1)
                    elif not first:
                        add(g - 1, UNITS - 1)
                    if not first:
                        finish_rows(g - 1, u)

            over_groups(pe, body)
            add(GROUPS - 1, UNITS - 1)
            pe.wait_ge(tail_w_landed, 5 * 16)
            for u in range(UNITS):
                finish_rows(GROUPS - 1, u)

        @block.vector
        def _(dve):
            def row_stats(xt, st, mv, step, base, done):
                for r in range(RB):
                    last = nc.vector.bn_stats(st[:, r, :], xt[:, r, :])
                last.then_inc(step, 1)
                dve.wait_ge(step, base + 1)
                nc.vector.memset(scratch[:], 0.0)
                for r in range(RB):
                    last = nc.vector.bn_aggr(mv[:, r, :], st[:, r, :])
                last.then_inc(done, 1)

            def normalise(xt, mv, rs, done):
                for r in range(RB):
                    last = nc.vector.tensor_scalar(h_n[:, r, :], xt[:, r, :], mv[:, r, 0:1], rs[:, r:r + 1],
                                                   ALU.subtract, ALU.mult)
                last.then_inc(done, 1)

            def stats_of(i, k):
                dve.wait_ge(x_landed[k], i * 16 + 16)
                row_stats(x_in[k], stats[k], mean_var[k], stat_step, i * 2 + k, stats_done)

            def save_nodes(t):
                dve.wait_ge(projected, t + 1)
                got = acc[0][:, 0:RB * (F + 2)].rearrange("p (r f) -> p r f", r=RB)
                nc.vector.tensor_copy(wh[:, bass.ds(t * RB, RB), 0:F], got[:, :, 0:F])
                nc.vector.tensor_copy(sd[:, :, bass.ds(t * RB, RB)],
                                      got[:, :, F:F + 2].rearrange("p r k -> p k r")).then_inc(wh_saved, 1)

            def pair(i, first=False, last=False):
                for k in range(2):
                    t = i * 2 + k
                    if not (last and k):
                        stats_of(i + k, 1 - k)
                    dve.wait_ge(rstd_done, t + 1)
                    dve.wait_ge(stats_done, t + 1)
                    if not (first and k == 0):
                        dve.wait_ge(h_flipped, t)
                    normalise(x_in[k], mean_var[k], rstd[k], normed)
                    if not (first and k == 0):
                        save_nodes(t - 1)

            dve.wait_ge(consts, CONSTS_ALL)
            stats_of(0, 0)
            over_pairs(dve, pair)
            save_nodes(GROUPS - 1)

            steps = [0]

            def node(ins):
                steps[0] += 1
                ins.then_inc(node_step, 1)
                dve.wait_ge(node_step, steps[0])

            dve.wait_ge(wh_saved, GROUPS)
            nc.vector.reduce_max(edge[:, 0:1], sd[:, 1, :], AX_X).then_inc(edges_local, 1)
            node(nc.vector.tensor_scalar(neg_d[:], sd[:, 1, :], -1.0, None, ALU.mult))
            nc.vector.reduce_max(edge[:, 1:2], neg_d[:], AX_X).then_inc(edges_local, 1)
            nc.vector.reduce_sum(wh_sum[:], wh[:, :, 0:F].rearrange("p n f -> p f n"), AX_X).then_inc(wh_summed, 1)
            node(nc.vector.tensor_scalar(steep_d[:], sd[:, 1, :], STEEP, None, ALU.mult))
            dve.wait_ge(edges_done, 1)
            node(nc.vector.tensor_scalar(d_shift[:], sd[:, 1, :], edge_all[:, 0:1], None, ALU.subtract))
            node(nc.vector.tensor_scalar(s_top[:], sd[:, 0, :], edge_all[:, 0:1], None, ALU.add))
            node(nc.vector.scalar_tensor_tensor(out=s_guard[:], in0=s_top[:], scalar=ALPHA, in1=s_top[:],
                                                op0=ALU.mult, op1=ALU.max))
            node(nc.vector.tensor_tensor(row_args[:, 0, :], s_top[:], s_guard[:], ALU.subtract))
            node(nc.vector.scalar_tensor_tensor(out=row_args[:, 1, :], in0=s_top[:], scalar=ALPHA,
                                                in1=s_guard[:], op0=ALU.mult, op1=ALU.subtract))
            assert steps[0] == NODE_STEPS
            dve.wait_ge(mean_ready, 1)
            nc.vector.tensor_copy(mean_row[:], tail[0][:, 0:F]).then_inc(mean_saved, 1)

            dve.wait_ge(scales_ready, 1)
            cuts = [0]

            def part(ins):
                cuts[0] += 1
                ins.then_inc(cut_step, 1)
                dve.wait_ge(cut_step, cuts[0])

            def cut_values(b):
                at = slice(b * BAT, (b + 1) * BAT)
                for k in range(2):
                    hi, mid, lo = (vals[k][:, at, n * FO:(n + 1) * FO] for n in range(PARTS))
                    part(nc.vector.tensor_tensor(cut[0][:], wh[:, at, :],
                                                 col_scale[:, k, at].unsqueeze(2).to_broadcast([P, BAT, FO]),
                                                 ALU.mult))
                    part(nc.vector.tensor_copy(hi, cut[0][:]))
                    part(nc.vector.tensor_tensor(cut[1][:], cut[0][:], hi, ALU.subtract))
                    part(nc.vector.tensor_copy(mid, cut[1][:]))
                    last = nc.vector.tensor_tensor(lo, cut[1][:], mid, ALU.subtract)
                    if k == 0:
                        part(last)
                    else:
                        last.then_inc(vals_ready, 1)
                        dve.wait_ge(vals_ready, b + 1)

            for b in range(JB // BAT):
                cut_values(b)

            def clean(g, c):
                dve.wait_ge(adj_landed[c % RING], (g * (CHUNKS // RING) + c // RING + 1) * 16)
                m = masks[c % RING]
                nc.vector.tensor_scalar(m[:], m[:], 0.0, 1.0, ALU.max, ALU.min).then_inc(mask_ready, 1)

            def take_rows(g):
                nc.vector.tensor_scalar(s_now[:], s_rows[:, bass.ds(g * ROWS, ROWS)], STEEP, None, ALU.mult)\
                    .then_inc(rows_taken, 1)

            def finish_rows(q, u):
                if u == 2:
                    dve.wait_ge(folded, q + 1)
                    got = tail[0][:, 0:RB * 2 * FO].rearrange("p (r k f) -> p r k f", r=RB, k=2)
                    n = [0]

                    def step(ins):
                        n[0] += 1
                        ins.then_inc(att_step, 1)
                        dve.wait_ge(att_step, q * ATT_STEPS + n[0])

                    for k in range(2):
                        step(nc.vector.tensor_tensor(
                            scaled[k][:], got[:, :, k, :],
                            row_scale[:, k, bass.ds(q * RB, RB)].unsqueeze(2).to_broadcast([P, RB, FO]),
                            ALU.mult))
                    step(nc.vector.tensor_tensor(total[:], scaled[0][:], scaled[1][:], ALU.add))
                    step(nc.vector.tensor_scalar(lonely[:], total[:, :, F], 0.0, None, ALU.is_equal))
                    nc.vector.tensor_tensor(lonely_mean[:], lonely[:].unsqueeze(2).to_broadcast([P, RB, F]),
                                            mean_row[:].unsqueeze(1).to_broadcast([P, RB, F]), ALU.mult)
                    step(nc.vector.tensor_tensor(denom[:], total[:, :, F], lonely[:], ALU.add))
                    step(nc.vector.reciprocal(inv_denom[:], denom[:]))
                    step(nc.vector.tensor_tensor(numer[:], total[:, :, 0:F], lonely_mean[:], ALU.add))
                    step(nc.vector.tensor_tensor(att[:], numer[:],
                                                 inv_denom[:].unsqueeze(2).to_broadcast([P, RB, F]), ALU.mult))
                    assert n[0] == ATT_STEPS
                if u == 5:
                    dve.wait_ge(proj_ready, q + 1)
                    dve.wait_ge(x_fcb_ready, q + 1)
                    for k in range(2):
                        rows = slice(k * RB // 2, (k + 1) * RB // 2)
                        last = nc.vector.tensor_tensor(x_mid[:, rows, :],
                                                       tail[k][:].rearrange("p (r d) -> p r d", d=DIM),
                                                       x_fcb[:, rows, :], ALU.add)
                    last.then_inc(x_mid_ready, 1)
                    dve.wait_ge(x_mid_ready, q + 1)
                    row_stats(x_mid, stats[0], mean_var[0], stats2_step, q, stats2_done)
                if u == 7:
                    dve.wait_ge(rstd2_done, q + 1)
                    dve.wait_ge(stats2_done, q + 1)
                    normalise(x_mid, mean_var[0], rstd[0], normed2)
                if u in (14, 15):
                    k = u - 14
                    rows = slice(k * RB // 2, (k + 1) * RB // 2)
                    dve.wait_ge(fc2_ready, q * 2 + k + 1)
                    dve.wait_ge(x_fc2b_ready, q + 1)
                    nc.vector.tensor_tensor(y_out[:, rows, :], tail[k][:].rearrange("p (r d) -> p r d", d=DIM),
                                            x_fc2b[:, rows, :], ALU.add).then_inc(y_ready, 1)

            def body(g, first=False, last=False):
                for u in range(UNITS):
                    if u % 2 == 0 and not (last and u == UNITS - 2):
                        c = u // 2 + 1
                        clean(g + c // CHUNKS, c % CHUNKS)
                    if u == UNITS - 1 and not last:
                        dve.wait_ge(above_ready, (g + 1) * UNITS)
                        take_rows(g + 1)
                    if not first:
                        finish_rows(g - 1, u)
                    U = g * UNITS + u
                    dve.wait_ge(unit_flipped, U + 1)
                    dve.wait_ge(above_ready, U + 1)
                    if not (first and u < 2):
                        dve.wait_ge(unit_added, U - 1)
                    nc.vector.tensor_tensor(pos[u % 2][:], above[u % 2][:], flipped[u % 2][:], ALU.min)\
                        .then_inc(pos_ready, 1)
                    dve.wait_ge(pos_ready, U + 1)
                    nc.vector.tensor_tensor(neg[u % 2][:], flipped[u % 2][:], pos[u % 2][:], ALU.subtract)\
                        .then_inc(neg_ready, 1)

            clean(0, 0)
            dve.wait_ge(s_saved, GROUPS)
            take_rows(0)
            over_groups(dve, body)
            for u in range(UNITS):
                finish_rows(GROUPS - 1, u)


def kernel(x, adj, L0_gnn_W, L0_gnn_a, L0_gnn_fc_w, L0_gnn_fc_b, L0_gnn_ln1_g, L0_gnn_ln1_b,
           L0_gnn_ln2_g, L0_gnn_ln2_b, L0_gnn_fc1_w, L0_gnn_fc1_b, L0_gnn_fc2_w, L0_gnn_fc2_b):
    import numpy as np
    import concourse.bacc as bacc
    from concourse.bass_utils import run_bass_kernel_spmd

    def columns(v):
        return np.asarray(v).reshape(-1, P).T

    laid = {
        "x": np.asarray(x),
        "adj": np.asarray(adj),
        "w": np.asarray(L0_gnn_W),
        "w_t": np.asarray(L0_gnn_W).T,
        "a_pair": np.asarray(L0_gnn_a).reshape(2, -1).T,
        "fc_t": np.asarray(L0_gnn_fc_w).T,
        "fc_b": np.asarray(L0_gnn_fc_b)[None, :],
        "ln1_gb": np.stack([columns(L0_gnn_ln1_g), columns(L0_gnn_ln1_b)], axis=1),
        "ln2_gb": np.stack([columns(L0_gnn_ln2_g), columns(L0_gnn_ln2_b)], axis=1),
        "fc1_t": np.asarray(L0_gnn_fc1_w).T,
        "fc1_b": columns(L0_gnn_fc1_b),
        "fc2_t": np.asarray(L0_gnn_fc2_w).T,
        "fc2_b": np.asarray(L0_gnn_fc2_b)[None, :],
    }
    nc = bacc.Bacc("TRN2", target_bir_lowering=False, num_devices=1)
    arrays, args = {}, []
    for name, v in laid.items():
        arrays[f"in_{name}"] = np.ascontiguousarray(v)
        args.append(nc.dram_tensor(f"in_{name}", v.shape, mybir.dt.from_np(v.dtype), kind="ExternalInput").ap())
    out = nc.dram_tensor("out", laid["x"].shape, F32, kind="ExternalOutput").ap()
    build_gat(nc, *args, out)
    r = run_bass_kernel_spmd(nc, [arrays], core_ids=[0])
    return r.results[0]["out"]
```

```python
from contextlib import ExitStack

import concourse.bass as bass
from concourse import mybir

F32 = mybir.dt.float32
BF16 = mybir.dt.bfloat16
ALU = mybir.AluOpType
ACT = mybir.ActivationFunctionType
AX_X = mybir.AxisListType.X
RMAX = bass.bass_isa.ReduceOp.max

P = 128
ALPHA = 0.2
EPS = 1e-5
PARTS = 3
STEEP = 2.0 ** 40


def build_gat(nc, x, adj, w, w_t, a_pair, fc_t, fc_b, ln1_gb, ln2_gb, fc1_t, fc1_b, fc2_t, fc2_b, out):
    N, DIM = x.shape
    F = w.shape[1]
    FO = F + 1
    HID = fc1_t.shape[1]
    KC = DIM // P
    HC = HID // P
    JB = N // P
    ROWS = 512
    RB = ROWS // P
    GROUPS = N // ROWS
    UNIT = 4
    UNITS = JB // UNIT
    CHUNKS = UNITS // 2
    CCOLS = N // CHUNKS
    X_RING = 4
    RING = 4
    AHEAD = RING - 1
    W3 = PARTS * FO
    CONSTS = 6
    CONSTS_ALL = CONSTS + PARTS + 2
    NODE_STEPS = 6
    ATT_STEPS = 8
    BAT = 16

    x_v = x.rearrange("(n p) d -> p n d", p=P)
    adj_v = adj.rearrange("(n p) j -> p n j", p=P)
    out_v = out.rearrange("(n p) d -> p n d", p=P)

    with ExitStack() as ctx:
        def sb(name, shape, dt=F32):
            return ctx.enter_context(nc.sbuf_tensor(name, shape, dt))

        def pb(name, shape, dt=F32):
            return ctx.enter_context(nc.psum_tensor(name, shape, dt))

        def sem(name):
            return ctx.enter_context(nc.semaphore(name))

        w_aug = sb("w_aug", [P, KC, F + 2])
        w_tr = sb("w_tr", [F, DIM])
        a_sd = sb("a_sd", [F, 2])
        fc_sb = sb("fc_sb", [F, DIM])
        fcb_row = sb("fcb_row", [P, DIM])
        fc2b_row = sb("fc2b_row", [P, DIM])
        ln1 = sb("ln1", [P, 2, KC])
        ln2 = sb("ln2", [P, 2, KC])
        fc1_sb = sb("fc1_sb", [P, KC, HID])
        fc1b = sb("fc1b", [P, HC])
        fc2_sb = sb("fc2_sb", [P, HC, DIM])
        ident = sb("ident", [P, P])
        identb = sb("identb", [P, P], BF16)
        ones_n = sb("ones_n", [P, P])
        fold3 = sb("fold3", [W3, FO])
        minus_half = sb("minus_half", [P, RB])
        eps = sb("eps", [P, RB])
        scratch = sb("scratch", [P, 1])

        wh = sb("wh", [P, JB, FO])
        sd = sb("sd", [P, 2, JB])
        s_rows = sb("s_rows", [P, N])
        s_now = sb("s_now", [P, ROWS])
        s_turned = sb("s_turned", [JB, P])
        steep_d = sb("steep_d", [P, JB])
        edge = sb("edge", [P, 2])
        edge_all = sb("edge_all", [P, 2])
        d_shift = sb("d_shift", [P, JB])
        s_top = sb("s_top", [P, JB])
        s_guard = sb("s_guard", [P, JB])
        row_args = sb("row_args", [P, 2, JB])
        row_scale = sb("row_scale", [P, 2, JB])
        col_scale = sb("col_scale", [P, 2, JB])
        wh_sum = sb("wh_sum", [P, F])
        mean_row = sb("mean_row", [P, F])
        vals = [sb(f"vals{k}", [P, JB, W3], BF16) for k in range(2)]
        cut = [sb(f"cut{k}", [P, BAT, FO]) for k in range(2)]

        masks = [sb(f"masks{k}", [P, RB, CCOLS], BF16) for k in range(RING)]
        above = [sb(f"above{k}", [P, UNIT, ROWS], BF16) for k in range(2)]
        pos = [sb(f"pos{k}", [P, UNIT, ROWS], BF16) for k in range(2)]
        neg = [sb(f"neg{k}", [P, UNIT, ROWS], BF16) for k in range(2)]

        sums = sb("sums", [W3, 2, ROWS])
        scaled = [sb(f"scaled{k}", [P, RB, FO]) for k in range(2)]
        total = sb("total", [P, RB, FO])
        lonely = sb("lonely", [P, RB])
        lonely_mean = sb("lonely_mean", [P, RB, F])
        denom = sb("denom", [P, RB])
        inv_denom = sb("inv_denom", [P, RB])
        numer = sb("numer", [P, RB, F])
        att = sb("att", [P, RB, F])
        att_t = sb("att_t", [F, ROWS])
        x_in = [sb(f"x_in{k}", [P, RB, DIM]) for k in range(2)]
        x_fcb = x_in[1]
        x_mid = sb("x_mid", [P, RB, DIM])
        x_fc2b = sb("x_fc2b", [P, RB, DIM])
        h_n = sb("h_n", [P, RB, DIM])
        h_t = sb("h_t", [P, KC, ROWS])
        act_t = sb("act_t", [P, HC, ROWS])
        y_out = sb("y_out", [P, RB, DIM])
        stats = [sb(f"stats{k}", [P, RB, 6]) for k in range(2)]
        mean_var = [sb(f"mean_var{k}", [P, RB, 2]) for k in range(2)]
        var_eps = sb("var_eps", [P, RB])
        rstd = [sb(f"rstd{k}", [P, RB]) for k in range(2)]

        flipped = [pb(f"flipped{k}", [P, UNIT, ROWS], BF16) for k in range(2)]
        acc = [pb(f"acc{k}", [P, ROWS]) for k in range(2)]
        tail = [pb(f"tail{k}", [P, ROWS]) for k in range(2)]

        pre_x = [x_in[0], x_in[1], x_mid, x_fc2b]
        pre_h = [h_n[:], y_out[:]]
        pre_t = [h_t[:], act_t[:, 0:KC, :]]
        spare = flipped[0][:].rearrange("p j r -> p (j r)").bitcast(F32)
        pre_tail = [[tail[c][:] for c in range(KC)], [spare[:, c * ROWS:(c + 1) * ROWS] for c in range(KC)]]
        s_dram = nc.dram_tensor("s_dram", [1, N], F32).ap()

        w_landed = sem("w_landed")
        gb_landed = sem("gb_landed")
        tail_w_landed = sem("tail_w_landed")
        x_landed = [sem(f"x_landed{k}") for k in range(X_RING)]
        consts = sem("consts")
        wa_ready = sem("wa_ready")
        wa_saved = sem("wa_saved")
        stat_step = sem("stat_step")
        stats_done = sem("stats_done")
        rstd_step = sem("rstd_step")
        rstd_done = sem("rstd_done")
        normed = sem("normed")
        h_flipped = sem("h_flipped")
        h_t_done = sem("h_t_done")
        projected = sem("projected")
        nodes_saved = sem("nodes_saved")
        s_flipped = sem("s_flipped")
        s_turned_ready = sem("s_turned_ready")
        s_written = sem("s_written")
        s_landed = [sem("s_landed_first"), sem("s_landed_rest")]
        node_step = sem("node_step")
        edges_local = sem("edges_local")
        edges_done = sem("edges_done")
        scales_ready = sem("scales_ready")
        wh_summed = sem("wh_summed")
        mean_ready = sem("mean_ready")
        mean_saved = sem("mean_saved")
        cut_step = sem("cut_step")
        vals_ready = sem("vals_ready")

        adj_landed = [sem(f"adj_landed{k}") for k in range(RING)]
        mask_ready = sem("mask_ready")
        chunk_flipped = sem("chunk_flipped")
        unit_flipped = sem("unit_flipped")
        rows_taken = sem("rows_taken")
        above_ready = sem("above_ready")
        pos_ready = sem("pos_ready")
        neg_ready = sem("neg_ready")
        unit_added = sem("unit_added")
        sums_saved = sem("sums_saved")
        folded = sem("folded")
        att_step = sem("att_step")
        att_flipped = sem("att_flipped")
        att_t_ready = sem("att_t_ready")
        proj_ready = sem("proj_ready")
        x_fcb_ready = sem("x_fcb_ready")
        x_mid_ready = sem("x_mid_ready")
        stats2_step = sem("stats2_step")
        stats2_done = sem("stats2_done")
        rstd2_step = sem("rstd2_step")
        rstd2_done = sem("rstd2_done")
        x_fc2b_ready = sem("x_fc2b_ready")
        normed2 = sem("normed2")
        h2_flipped = sem("h2_flipped")
        h2_t_done = sem("h2_t_done")
        fc1_ready = sem("fc1_ready")
        gelu_done = sem("gelu_done")
        fc2_ready = sem("fc2_ready")
        y_ready = sem("y_ready")
        y_stored = sem("y_stored")
        x2_landed = sem("x2_landed")

        def over_groups(eng, body):
            body(0, first=True)
            with eng.Fori(1, GROUPS - 1) as g:
                body(g)
            body(GROUPS - 1, last=True)

        def over_turns(eng, body):
            body(0, first=True)
            with eng.Fori(1, GROUPS // X_RING - 1) as i:
                body(i)
            body(GROUPS // X_RING - 1, last=True)

        block = ctx.enter_context(nc.Block())

        @block.sync
        def _(sp):
            def load_x(to, n):
                return sp.dma_start(to[:], x_v[:, bass.ds(n * RB, RB), :])

            load_x(pre_x[0], 0).then_inc(x_landed[0], 16)
            sp.dma_start(w_aug[:, :, 0:F], w.rearrange("(c p) f -> p c f", p=P)).then_inc(w_landed, 16)
            sp.dma_start(w_tr[:], w_t).then_inc(w_landed, 16)
            sp.dma_start(a_sd[:], a_pair).then_inc(w_landed, 16)
            for k in range(1, X_RING):
                load_x(pre_x[k], k).then_inc(x_landed[k], 16)
            sp.dma_start(ln1[:], ln1_gb).then_inc(gb_landed, 16)
            sp.dma_start(ln2[:], ln2_gb).then_inc(gb_landed, 16)
            sp.dma_start(fc1b[:], fc1_b).then_inc(gb_landed, 16)
            sp.dma_start(fc_sb[:], fc_t).then_inc(tail_w_landed, 16)
            sp.dma_start(fc1_sb[:], fc1_t.rearrange("(c p) h -> p c h", p=P)).then_inc(tail_w_landed, 16)
            sp.dma_start(fc2_sb[:], fc2_t.rearrange("(c p) d -> p c d", p=P)).then_inc(tail_w_landed, 16)
            sp.dma_start(fcb_row[:], fc_b.to_broadcast([P, DIM])).then_inc(tail_w_landed, 16)
            sp.dma_start(fc2b_row[:], fc2_b.to_broadcast([P, DIM])).then_inc(tail_w_landed, 16)

            with sp.Fori(1, GROUPS // X_RING) as i:
                for k in range(X_RING):
                    sp.wait_ge(normed, (i - 1) * X_RING + k + 1)
                    load_x(pre_x[k], i * X_RING + k).then_inc(x_landed[k], 16)

            def store(q, part):
                half = RB // 2
                sp.wait_ge(y_ready, q * 2 + part + 1)
                sp.dma_start(out_v[:, bass.ds(q * RB + part * half, half), :],
                             y_out[:, part * half:(part + 1) * half, :]).then_inc(y_stored, 16)

            def finish(q, first=False):
                if not first:
                    sp.wait_ge(x_fcb_ready, q)
                    sp.wait_ge(y_stored, q * 2 * 16)
                load_x(x_in[0], q).then_inc(x2_landed, 16)
                store(q, 0)
                store(q, 1)

            sp.wait_ge(s_turned_ready, 1)
            sp.dma_start(s_dram.rearrange("a (b p) -> (a b) p", p=P), s_turned[:]).then_inc(s_written, 16)
            sp.wait_ge(s_written, 16)
            for k, at in enumerate((slice(0, ROWS), slice(ROWS, N))):
                sp.dma_start(s_rows[:, at], s_dram[:, at].to_broadcast([P, at.stop - at.start]))\
                    .then_inc(s_landed[k], 16)

            finish(0, first=True)
            with sp.Fori(1, GROUPS) as q:
                finish(q)
            sp.wait_ge(y_stored, 16 * 2 * GROUPS)

        @block.gpsimd
        def _(pool):
            def load_chunk(g, c):
                pool.dma_start(masks[c % RING][:], adj_v[:, bass.ds(g * RB, RB), c * CCOLS:(c + 1) * CCOLS])\
                    .then_inc(adj_landed[c % RING], 16)

            for c in range(AHEAD):
                load_chunk(0, c)

            nc.gpsimd.memset(ident[:], 0.0).then_inc(consts, 1)
            nc.gpsimd.memset(fold3[:], 0.0).then_inc(consts, 1)
            nc.gpsimd.memset(minus_half[:], -0.5).then_inc(consts, 1)
            nc.gpsimd.memset(eps[:], EPS).then_inc(consts, 1)
            nc.gpsimd.memset(wh[:], 1.0).then_inc(consts, 1)
            nc.gpsimd.memset(ones_n[:], 1.0 / N).then_inc(consts, 1)
            pool.wait_ge(consts, CONSTS)
            nc.gpsimd.affine_select(out=ident[:], in_=ident[:], compare_op=ALU.not_equal, fill=1.0,
                                    base=0, pattern=[[-1, P]], channel_multiplier=1).then_inc(consts, 1)
            for part in range(PARTS):
                nc.gpsimd.affine_select(out=fold3[:], in_=fold3[:], compare_op=ALU.not_equal, fill=1.0,
                                        base=-part * FO, pattern=[[-1, FO]], channel_multiplier=1)\
                    .then_inc(consts, 1)
                pool.wait_ge(consts, CONSTS + 2 + part)
            nc.gpsimd.tensor_copy(identb[:], ident[:]).then_inc(consts, 1)

            def inverse_deviation(step, base, mv, to, done):
                nc.gpsimd.tensor_tensor(var_eps[:], mv[:, :, 1], eps[:], ALU.add).then_inc(step, 1)
                pool.wait_ge(step, base + 1)
                nc.gpsimd.tensor_tensor(to[:], var_eps[:], minus_half[:], ALU.pow).then_inc(done, 1)
                pool.wait_ge(done, base + 1)

            with pool.Fori(0, GROUPS // X_RING) as i:
                for k in range(X_RING):
                    t = i * X_RING + k
                    pool.wait_ge(stats_done, t + 1)
                    inverse_deviation(rstd_step, t, mean_var[k % 2], rstd[k % 2], rstd_done)

            pool.wait_ge(edges_local, 2)
            nc.gpsimd.partition_all_reduce(edge_all[:], edge[:], P, RMAX).then_inc(edges_done, 1)

            pool.wait_ge(tail_w_landed, 5 * 16)

            def body(g, first=False, last=False):
                q = g - 1
                for c in range(CHUNKS):
                    if not (last and c + AHEAD >= CHUNKS):
                        if not (first and c == 0):
                            pool.wait_ge(chunk_flipped, g * CHUNKS + c)
                        ahead = c + AHEAD
                        load_chunk(g + ahead // CHUNKS, ahead % CHUNKS)
                    if not first:
                        finish_rows(q, c)

            def finish_rows(q, c):
                if c == 0:
                    pool.wait_ge(x2_landed, 16 * (q + 1))
                    nc.gpsimd.tensor_tensor(x_fcb[:], x_in[0][:],
                                            fcb_row[:].unsqueeze(1).to_broadcast([P, RB, DIM]),
                                            ALU.add).then_inc(x_fcb_ready, 1)
                if c == 2:
                    pool.wait_ge(stats2_done, q + 1)
                    inverse_deviation(rstd2_step, q, mean_var[0], rstd[0], rstd2_done)
                    pool.wait_ge(x_mid_ready, q + 1)
                    nc.gpsimd.tensor_tensor(x_fc2b[:], x_mid[:],
                                            fc2b_row[:].unsqueeze(1).to_broadcast([P, RB, DIM]),
                                            ALU.add).then_inc(x_fc2b_ready, 1)

            over_groups(pool, body)
            for c in range(CHUNKS):
                finish_rows(GROUPS - 1, c)

        def affine_flip(to, got, gb, ready):
            for c in range(KC):
                last = nc.scalar.activation(to[:, c, :], got[c], ACT.Identity,
                                            bias=gb[:, 1, c:c + 1], scale=gb[:, 0, c:c + 1])
            last.then_inc(ready, 1)

        @block.scalar
        def _(act):
            act.wait_ge(gb_landed, 3 * 16)
            act.wait_ge(wa_ready, 1)
            for c in range(KC):
                last = nc.scalar.activation(w_aug[:, c, F:F + 2], acc[1][:, 2 * c:2 * c + 2], ACT.Copy)
            last.then_inc(wa_saved, 1)

            def save_nodes(t, k):
                got = acc[k][:, 0:RB * (F + 2)].rearrange("p (r f) -> p r f", r=RB)
                nc.scalar.activation(wh[:, bass.ds(t * RB, RB), 0:F], got[:, :, 0:F], ACT.Copy)
                nc.scalar.activation(sd[:, :, bass.ds(t * RB, RB)],
                                     got[:, :, F:F + 2].rearrange("p r k -> p k r"), ACT.Copy)\
                    .then_inc(nodes_saved, 1)

            act.wait_ge(consts, CONSTS_ALL)

            def turn(i, first=False, last=False):
                for k in range(X_RING):
                    t = i * X_RING + k
                    if not (first and k == 0):
                        act.wait_ge(projected, t)
                    act.wait_ge(h_flipped, t + 1)
                    affine_flip(pre_t[k % 2], pre_tail[k % 2], ln1, h_t_done)
                    if not (first and k == 0):
                        save_nodes(t - 1, (k - 1) % 2)

            over_turns(act, turn)
            act.wait_ge(projected, GROUPS)
            save_nodes(GROUPS - 1, 1)

            act.wait_ge(s_flipped, 1)
            nc.scalar.activation(s_turned[:], tail[1][0:JB, 0:P], ACT.Copy).then_inc(s_turned_ready, 1)

            act.wait_ge(node_step, NODE_STEPS)
            nc.scalar.activation(col_scale[:, 0, :], d_shift[:], ACT.Exp)
            nc.scalar.activation(col_scale[:, 1, :], d_shift[:], ACT.Exp, scale=ALPHA)
            nc.scalar.activation(row_scale[:], row_args[:], ACT.Exp).then_inc(scales_ready, 1)
            nc.scalar.preload_act_table(ACT.Gelu)

            def mark(g, u):
                for j in range(UNIT):
                    jb = u * UNIT + j
                    last = nc.scalar.activation(above[u % 2][:, j, :], s_now[:],
                                                ACT.Relu, bias=steep_d[:, jb:jb + 1])
                last.then_inc(above_ready, 1)

            def finish_rows(q, u):
                if u == 0:
                    act.wait_ge(unit_added, (q + 1) * UNITS)
                    for k in range(2):
                        last = nc.scalar.activation(sums[:, k, :], acc[k][0:W3, :], ACT.Copy)
                    last.then_inc(sums_saved, 1)
                if u == 3:
                    act.wait_ge(att_flipped, q + 1)
                    nc.scalar.activation(att_t[:], tail[1][0:F, :], ACT.Copy).then_inc(att_t_ready, 1)
                if u == 7:
                    act.wait_ge(h2_flipped, q + 1)
                    affine_flip(h_t, [t[:] for t in tail], ln2, h2_t_done)
                if 8 <= u < 8 + HC:
                    m = u - 8
                    act.wait_ge(fc1_ready, q * HC + m + 1)
                    nc.scalar.activation(act_t[:, m, :], tail[m % 2][:], ACT.Gelu,
                                         bias=fc1b[:, m:m + 1]).then_inc(gelu_done, 1)

            def body(g, first=False, last=False):
                for u in range(UNITS):
                    if not (last and u == UNITS - 1):
                        if u == UNITS - 1:
                            act.wait_ge(rows_taken, g + 2)
                        if not (first and u == 0):
                            act.wait_ge(pos_ready, g * UNITS + u)
                        nxt = u + 1
                        mark(g + nxt // UNITS, nxt % UNITS)
                    if not first:
                        finish_rows(g - 1, u)

            act.wait_ge(rows_taken, 1)
            mark(0, 0)
            over_groups(act, body)
            for u in range(UNITS):
                finish_rows(GROUPS - 1, u)

        @block.tensor
        def _(pe):
            pe.wait_ge(w_landed, 3 * 16)
            for c in range(KC):
                last = nc.tensor.matmul(acc[1][:, 2 * c:2 * c + 2], w_tr[:, c * P:(c + 1) * P], a_sd[:],
                                        start=True, stop=True)
            last.then_inc(wa_ready, 1)
            pe.wait_ge(consts, CONSTS_ALL)
            pe.wait_ge(wa_saved, 1)

            def flip_rows(rows, to, done):
                for c in range(KC):
                    for r in range(RB):
                        last = nc.tensor.transpose(to[c][:, r * P:(r + 1) * P],
                                                   rows[:, r, c * P:(c + 1) * P], ident[:])
                last.then_inc(done, 1)

            def flip_group(t, k, free=None):
                pe.wait_ge(normed, t + 1)
                if free is not None:
                    pe.wait_ge(h_t_done, free)
                flip_rows(pre_h[k], pre_tail[k], h_flipped)

            def project(t, k, free=None):
                pe.wait_ge(h_t_done, t + 1)
                if free is not None:
                    pe.wait_ge(nodes_saved, free)
                for r in range(RB):
                    for c in range(KC):
                        last = nc.tensor.matmul(acc[k][:, r * (F + 2):(r + 1) * (F + 2)],
                                                pre_t[k][:, c, r * P:(r + 1) * P], w_aug[:, c, :],
                                                start=(c == 0), stop=(c == KC - 1))
                last.then_inc(projected, 1)

            def turn(i, first=False, last=False):
                for k in range(X_RING):
                    t = i * X_RING + k
                    if not (last and k == X_RING - 1):
                        flip_group(t + 1, (k + 1) % 2, None if first and k == 0 else t)
                    project(t, k % 2, None if first and k < 2 else t - 1)

            flip_group(0, 0)
            over_turns(pe, turn)

            pe.wait_ge(nodes_saved, GROUPS)
            nc.tensor.transpose(tail[1][0:JB, 0:P], sd[:, 0, :], ident[:]).then_inc(s_flipped, 1)
            pe.wait_ge(wh_summed, 1)
            nc.tensor.matmul(tail[0][:, 0:F], ones_n[:], wh_sum[:], start=True, stop=True).then_inc(mean_ready, 1)
            pe.wait_ge(mean_saved, 1)

            def flip(g, u):
                c = u // 2
                if u % 2 == 0:
                    pe.wait_ge(mask_ready, g * CHUNKS + c + 1)
                for j in range(UNIT):
                    col = (u % 2 * UNIT + j) * P
                    for r in range(RB):
                        last = nc.tensor.transpose(flipped[u % 2][:, j, r * P:(r + 1) * P],
                                                   masks[c % RING][:, r, col:col + P], identb[:])
                last.then_inc(unit_flipped, 1)
                if u % 2:
                    pe.wait_ge(unit_flipped, g * UNITS + u + 1)
                    pe.sem_inc(chunk_flipped, 1)

            def add(g, u):
                for k, side, ready in ((0, pos, pos_ready), (1, neg, neg_ready)):
                    pe.wait_ge(ready, g * UNITS + u + 1)
                    for j in range(UNIT):
                        jb = u * UNIT + j
                        last = nc.tensor.matmul(acc[k][0:W3, :], vals[k][:, jb, :], side[u % 2][:, j, :],
                                                start=(jb == 0), stop=(jb == JB - 1))
                last.then_inc(unit_added, 1)

            def finish_rows(q, u):
                if u == 1:
                    pe.wait_ge(sums_saved, q + 1)
                    for r in range(RB):
                        for k in range(2):
                            last = nc.tensor.matmul(tail[0][:, (2 * r + k) * FO:(2 * r + k + 1) * FO],
                                                    sums[:, k, r * P:(r + 1) * P], fold3[:],
                                                    start=True, stop=True)
                    last.then_inc(folded, 1)
                if u == 3:
                    pe.wait_ge(att_step, (q + 1) * ATT_STEPS)
                    for r in range(RB):
                        last = nc.tensor.transpose(tail[1][0:F, r * P:(r + 1) * P], att[:, r, :], ident[:])
                    last.then_inc(att_flipped, 1)
                if u == 4:
                    pe.wait_ge(att_t_ready, q + 1)
                    for r in range(RB):
                        last = nc.tensor.matmul(tail[r // 2][:, r % 2 * DIM:(r % 2 + 1) * DIM],
                                                att_t[:, r * P:(r + 1) * P], fc_sb[:], start=True, stop=True)
                    last.then_inc(proj_ready, 1)
                if u == 7:
                    pe.wait_ge(normed2, q + 1)
                    flip_rows(h_n, tail, h2_flipped)
                if 8 <= u < 8 + HC:
                    m = u - 8
                    pe.wait_ge(h2_t_done, q + 1)
                    if m >= 2:
                        pe.wait_ge(gelu_done, q * HC + m - 1)
                    for c in range(KC):
                        last = nc.tensor.matmul(tail[m % 2][:], fc1_sb[:, c, m * P:(m + 1) * P], h_t[:, c, :],
                                                start=(c == 0), stop=(c == KC - 1))
                    last.then_inc(fc1_ready, 1)
                if 12 <= u < 15:
                    pe.wait_ge(gelu_done, (q + 1) * HC)
                    for r in ((0,), (1,), (2, 3))[u - 12]:
                        for m in range(HC):
                            last = nc.tensor.matmul(tail[r // 2][:, r % 2 * DIM:(r % 2 + 1) * DIM],
                                                    act_t[:, m, r * P:(r + 1) * P], fc2_sb[:, m, :],
                                                    start=(m == 0), stop=(m == HC - 1))
                    if u > 12:
                        last.then_inc(fc2_ready, 1)

            def body(g, first=False, last=False):
                for u in range(UNITS):
                    if not (first and u < 2):
                        pe.wait_ge(neg_ready, g * UNITS + u - 1)
                    flip(g, u)
                    if u > 0:
                        if u == 1 and not first:
                            pe.wait_ge(sums_saved, g)
                        if first and (u - 1) % (BAT // UNIT) == 0:
                            pe.wait_ge(vals_ready, (u - 1) // (BAT // UNIT) + 1)
                        add(g, u - 1)
                    elif not first:
                        add(g - 1, UNITS - 1)
                    if not first:
                        finish_rows(g - 1, u)

            over_groups(pe, body)
            add(GROUPS - 1, UNITS - 1)
            pe.wait_ge(tail_w_landed, 5 * 16)
            for u in range(UNITS):
                finish_rows(GROUPS - 1, u)

        @block.vector
        def _(dve):
            def row_stats(xt, st, mv, step, base, done):
                for r in range(RB):
                    last = nc.vector.bn_stats(st[:, r, :], xt[:, r, :])
                last.then_inc(step, 1)
                dve.wait_ge(step, base + 1)
                nc.vector.memset(scratch[:], 0.0)
                for r in range(RB):
                    last = nc.vector.bn_aggr(mv[:, r, :], st[:, r, :])
                last.then_inc(done, 1)

            def normalise(xt, to, mv, rs, done):
                for r in range(RB):
                    last = nc.vector.tensor_scalar(to[:, r, :], xt[:, r, :], mv[:, r, 0:1], rs[:, r:r + 1],
                                                   ALU.subtract, ALU.mult)
                last.then_inc(done, 1)

            def stats_of(i, k):
                dve.wait_ge(x_landed[k], i * 16 + 16)
                row_stats(pre_x[k], stats[k % 2], mean_var[k % 2], stat_step, i * X_RING + k, stats_done)

            def turn(i, first=False, last=False):
                for k in range(X_RING):
                    t = i * X_RING + k
                    if not (last and k == X_RING - 1):
                        stats_of(i + (k + 1) // X_RING, (k + 1) % X_RING)
                    dve.wait_ge(rstd_done, t + 1)
                    dve.wait_ge(stats_done, t + 1)
                    if not (first and k < 2):
                        dve.wait_ge(h_flipped, t - 1)
                    normalise(pre_x[k], pre_h[k % 2], mean_var[k % 2], rstd[k % 2], normed)

            dve.wait_ge(consts, CONSTS_ALL)
            stats_of(0, 0)
            over_turns(dve, turn)

            steps = [0]

            def node(ins):
                steps[0] += 1
                ins.then_inc(node_step, 1)
                dve.wait_ge(node_step, steps[0])

            dve.wait_ge(nodes_saved, GROUPS)
            nc.vector.reduce_max(edge[:, 0:1], sd[:, 1, :], AX_X).then_inc(edges_local, 1)
            nc.vector.tensor_reduce(edge[:, 1:2], sd[:, 1, :], AX_X, ALU.min, negate=True)\
                .then_inc(edges_local, 1)
            nc.vector.reduce_sum(wh_sum[:], wh[:, :, 0:F].rearrange("p n f -> p f n"), AX_X).then_inc(wh_summed, 1)
            node(nc.vector.tensor_scalar(steep_d[:], sd[:, 1, :], STEEP, None, ALU.mult))
            dve.wait_ge(edges_done, 1)
            node(nc.vector.tensor_scalar(d_shift[:], sd[:, 1, :], edge_all[:, 0:1], None, ALU.subtract))
            node(nc.vector.tensor_scalar(s_top[:], sd[:, 0, :], edge_all[:, 0:1], None, ALU.add))
            node(nc.vector.scalar_tensor_tensor(out=s_guard[:], in0=s_top[:], scalar=ALPHA, in1=s_top[:],
                                                op0=ALU.mult, op1=ALU.max))
            node(nc.vector.tensor_tensor(row_args[:, 0, :], s_top[:], s_guard[:], ALU.subtract))
            node(nc.vector.scalar_tensor_tensor(out=row_args[:, 1, :], in0=s_top[:], scalar=ALPHA,
                                                in1=s_guard[:], op0=ALU.mult, op1=ALU.subtract))
            assert steps[0] == NODE_STEPS
            dve.wait_ge(mean_ready, 1)
            nc.vector.tensor_copy(mean_row[:], tail[0][:, 0:F]).then_inc(mean_saved, 1)

            dve.wait_ge(scales_ready, 1)
            cuts = [0]

            def part(ins):
                cuts[0] += 1
                ins.then_inc(cut_step, 1)
                dve.wait_ge(cut_step, cuts[0])

            def cut_values(b):
                at = slice(b * BAT, (b + 1) * BAT)
                for k in range(2):
                    hi, mid, lo = (vals[k][:, at, n * FO:(n + 1) * FO] for n in range(PARTS))
                    part(nc.vector.tensor_tensor(cut[0][:], wh[:, at, :],
                                                 col_scale[:, k, at].unsqueeze(2).to_broadcast([P, BAT, FO]),
                                                 ALU.mult))
                    part(nc.vector.tensor_copy(hi, cut[0][:]))
                    part(nc.vector.tensor_tensor(cut[1][:], cut[0][:], hi, ALU.subtract))
                    part(nc.vector.tensor_copy(mid, cut[1][:]))
                    last = nc.vector.tensor_tensor(lo, cut[1][:], mid, ALU.subtract)
                    if k == 0:
                        part(last)
                    else:
                        last.then_inc(vals_ready, 1)
                        dve.wait_ge(vals_ready, b + 1)

            cut_values(0)

            def clean(g, c):
                dve.wait_ge(adj_landed[c % RING], (g * (CHUNKS // RING) + c // RING + 1) * 16)
                m = masks[c % RING]
                nc.vector.tensor_scalar(m[:], m[:], 0.0, 1.0, ALU.max, ALU.min).then_inc(mask_ready, 1)

            def take_rows(g):
                nc.vector.tensor_scalar(s_now[:], s_rows[:, bass.ds(g * ROWS, ROWS)], STEEP, None, ALU.mult)\
                    .then_inc(rows_taken, 1)

            def finish_rows(q, u):
                if u == 2:
                    dve.wait_ge(folded, q + 1)
                    got = tail[0][:, 0:RB * 2 * FO].rearrange("p (r k f) -> p r k f", r=RB, k=2)
                    n = [0]

                    def step(ins):
                        n[0] += 1
                        ins.then_inc(att_step, 1)
                        dve.wait_ge(att_step, q * ATT_STEPS + n[0])

                    for k in range(2):
                        step(nc.vector.tensor_tensor(
                            scaled[k][:], got[:, :, k, :],
                            row_scale[:, k, bass.ds(q * RB, RB)].unsqueeze(2).to_broadcast([P, RB, FO]),
                            ALU.mult))
                    step(nc.vector.tensor_tensor(total[:], scaled[0][:], scaled[1][:], ALU.add))
                    step(nc.vector.tensor_scalar(lonely[:], total[:, :, F], 0.0, None, ALU.is_equal))
                    nc.vector.tensor_tensor(lonely_mean[:], lonely[:].unsqueeze(2).to_broadcast([P, RB, F]),
                                            mean_row[:].unsqueeze(1).to_broadcast([P, RB, F]), ALU.mult)
                    step(nc.vector.tensor_tensor(denom[:], total[:, :, F], lonely[:], ALU.add))
                    step(nc.vector.reciprocal(inv_denom[:], denom[:]))
                    step(nc.vector.tensor_tensor(numer[:], total[:, :, 0:F], lonely_mean[:], ALU.add))
                    step(nc.vector.tensor_tensor(att[:], numer[:],
                                                 inv_denom[:].unsqueeze(2).to_broadcast([P, RB, F]), ALU.mult))
                    assert n[0] == ATT_STEPS
                if u == 5:
                    dve.wait_ge(proj_ready, q + 1)
                    dve.wait_ge(x_fcb_ready, q + 1)
                    for k in range(2):
                        rows = slice(k * RB // 2, (k + 1) * RB // 2)
                        last = nc.vector.tensor_tensor(x_mid[:, rows, :],
                                                       tail[k][:].rearrange("p (r d) -> p r d", d=DIM),
                                                       x_fcb[:, rows, :], ALU.add)
                    last.then_inc(x_mid_ready, 1)
                    dve.wait_ge(x_mid_ready, q + 1)
                    row_stats(x_mid, stats[0], mean_var[0], stats2_step, q, stats2_done)
                if u == 7:
                    dve.wait_ge(rstd2_done, q + 1)
                    dve.wait_ge(stats2_done, q + 1)
                    normalise(x_mid, h_n, mean_var[0], rstd[0], normed2)
                if u in (14, 15):
                    k = u - 14
                    rows = slice(k * RB // 2, (k + 1) * RB // 2)
                    dve.wait_ge(fc2_ready, q * 2 + k + 1)
                    dve.wait_ge(x_fc2b_ready, q + 1)
                    nc.vector.tensor_tensor(y_out[:, rows, :], tail[k][:].rearrange("p (r d) -> p r d", d=DIM),
                                            x_fc2b[:, rows, :], ALU.add).then_inc(y_ready, 1)

            def body(g, first=False, last=False):
                for u in range(UNITS):
                    if u % 2 == 0 and not (last and u == UNITS - 2):
                        c = u // 2 + 1
                        clean(g + c // CHUNKS, c % CHUNKS)
                    if first and u % (BAT // UNIT) == 0 and u + BAT // UNIT < UNITS:
                        cut_values(u * UNIT // BAT + 1)
                    if first and u == UNITS - 1:
                        dve.wait_ge(s_landed[1], 16)
                    if u == UNITS - 1 and not last:
                        dve.wait_ge(above_ready, (g + 1) * UNITS)
                        take_rows(g + 1)
                    if not first:
                        finish_rows(g - 1, u)
                    U = g * UNITS + u
                    dve.wait_ge(unit_flipped, U + 1)
                    dve.wait_ge(above_ready, U + 1)
                    if not (first and u < 2):
                        dve.wait_ge(unit_added, U - 1)
                    nc.vector.tensor_tensor(pos[u % 2][:], above[u % 2][:], flipped[u % 2][:], ALU.min)\
                        .then_inc(pos_ready, 1)
                    dve.wait_ge(pos_ready, U + 1)
                    nc.vector.tensor_tensor(neg[u % 2][:], flipped[u % 2][:], pos[u % 2][:], ALU.subtract)\
                        .then_inc(neg_ready, 1)

            clean(0, 0)
            dve.wait_ge(s_landed[0], 16)
            take_rows(0)
            over_groups(dve, body)
            for u in range(UNITS):
                finish_rows(GROUPS - 1, u)


def kernel(x, adj, L0_gnn_W, L0_gnn_a, L0_gnn_fc_w, L0_gnn_fc_b, L0_gnn_ln1_g, L0_gnn_ln1_b,
           L0_gnn_ln2_g, L0_gnn_ln2_b, L0_gnn_fc1_w, L0_gnn_fc1_b, L0_gnn_fc2_w, L0_gnn_fc2_b):
    import numpy as np
    import concourse.bacc as bacc
    from concourse.bass_utils import run_bass_kernel_spmd

    def columns(v):
        return np.asarray(v).reshape(-1, P).T

    laid = {
        "x": np.asarray(x),
        "adj": np.asarray(adj),
        "w": np.asarray(L0_gnn_W),
        "w_t": np.asarray(L0_gnn_W).T,
        "a_pair": np.asarray(L0_gnn_a).reshape(2, -1).T,
        "fc_t": np.asarray(L0_gnn_fc_w).T,
        "fc_b": np.asarray(L0_gnn_fc_b)[None, :],
        "ln1_gb": np.stack([columns(L0_gnn_ln1_g), columns(L0_gnn_ln1_b)], axis=1),
        "ln2_gb": np.stack([columns(L0_gnn_ln2_g), columns(L0_gnn_ln2_b)], axis=1),
        "fc1_t": np.asarray(L0_gnn_fc1_w).T,
        "fc1_b": columns(L0_gnn_fc1_b),
        "fc2_t": np.asarray(L0_gnn_fc2_w).T,
        "fc2_b": np.asarray(L0_gnn_fc2_b)[None, :],
    }
    nc = bacc.Bacc("TRN2", target_bir_lowering=False, num_devices=1)
    arrays, args = {}, []
    for name, v in laid.items():
        arrays[f"in_{name}"] = np.ascontiguousarray(v)
        args.append(nc.dram_tensor(f"in_{name}", v.shape, mybir.dt.from_np(v.dtype), kind="ExternalInput").ap())
    out = nc.dram_tensor("out", laid["x"].shape, F32, kind="ExternalOutput").ap()
    build_gat(nc, *args, out)
    r = run_bass_kernel_spmd(nc, [arrays], core_ids=[0])
    return r.results[0]["out"]
```

```python
from contextlib import ExitStack

import concourse.bass as bass
from concourse import mybir

F32 = mybir.dt.float32
BF16 = mybir.dt.bfloat16
ALU = mybir.AluOpType
ACT = mybir.ActivationFunctionType
AX_X = mybir.AxisListType.X
RMAX = bass.bass_isa.ReduceOp.max

P = 128
ALPHA = 0.2
EPS = 1e-5
PARTS = 3
WIDE = 60.0
TINY = 1e-30
MASKED = -9e15
STEEP = 2.0 ** 40


def build_gat(nc, x, x_t, adj, w, w_t, a_pair, fc_t, fc_b, ln1_gb, ln2_gb, fc1_t, fc1_b, fc2_t, fc2_b, out):
    N, DIM = x.shape
    F = w.shape[1]
    FO = F + 1
    HID = fc1_t.shape[1]
    KC = DIM // P
    HC = HID // P
    JB = N // P
    ROWS = 512
    RB = ROWS // P
    GROUPS = N // ROWS
    UNIT = 4
    UNITS = JB // UNIT
    CHUNKS = UNITS // 2
    CCOLS = N // CHUNKS
    X_RING = 4
    NODE = FO + 2
    RING = 4
    AHEAD = RING - 1
    W3 = PARTS * FO
    CONSTS = 8
    CONSTS_ALL = CONSTS + PARTS + 2
    NODE_STEPS = 6
    CLEAN_AT = {0: 1, 2: 2, 4: 3, 7: 4, 8: 5, 10: 6, 12: 7, 14: 8}
    NORM_AT = 6
    FINISH_FIRST = (4,)
    MEAN_PIECES = JB * F // ROWS
    MEAN_AT = 5
    ATT_STEPS = 6
    DENSE_ATT_STEP = 1
    CUTS = ((0, 4), (4, 8), (8, 16), (16, 32), (32, 48), (48, 64))
    CUT_AT_UNIT = {1: 1, 2: 2, 3: 3, 6: 4}
    CUT_AT_CHUNK = {0: ((1, 1), (1, 2)), 1: ((1, 3),), 3: ((1, 4),), 4: ((1, 5),), 5: ((0, 5),)}
    CUT_MAX = 16
    assert CUTS[-1][1] == JB

    x_v = x.rearrange("(n p) d -> p n d", p=P)
    x_t_v = x_t.rearrange("(c p) n -> p c n", p=P)
    adj_v = adj.rearrange("(n p) j -> p n j", p=P)
    out_v = out.rearrange("(n p) d -> p n d", p=P)

    with ExitStack() as ctx:
        def sb(name, shape, dt=F32):
            return ctx.enter_context(nc.sbuf_tensor(name, shape, dt))

        def pb(name, shape, dt=F32):
            return ctx.enter_context(nc.psum_tensor(name, shape, dt))

        def sem(name):
            return ctx.enter_context(nc.semaphore(name))

        w_aug = sb("w_aug", [P, KC, NODE])
        w_g = sb("w_g", [P, KC, NODE])
        c_row = sb("c_row", [P, NODE])
        b_row = sb("b_row", [P, NODE])
        w_tr = sb("w_tr", [F, DIM])
        a_sd = sb("a_sd", [F, 2])
        fc_sb = sb("fc_sb", [F, DIM])
        fcb_row = sb("fcb_row", [P, DIM])
        fc2b_row = sb("fc2b_row", [P, DIM])
        ln1 = sb("ln1", [P, 2, KC])
        ln2 = sb("ln2", [P, 2, KC])
        fc1_sb = sb("fc1_sb", [P, KC, HID])
        fc1b = sb("fc1b", [P, HC])
        fc2_sb = sb("fc2_sb", [P, HC, DIM])
        ident = sb("ident", [P, P])
        identb = sb("identb", [P, P], BF16)
        ones_n = sb("ones_n", [P, P])
        minus_ones = sb("minus_ones", [P, P])
        fold3 = sb("fold3", [W3, FO])
        minus_half = sb("minus_half", [P, RB])
        eps = sb("eps", [P, RB])
        scratch = sb("scratch", [P, 1])
        f_dst_range = sb("f_dst_range", [P, 1])
        wide = sb("wide", [P, 1])

        nodes = sb("nodes", [P, JB, NODE])
        wh = nodes[:, :, 0:FO]
        f_src = nodes[:, :, FO]
        f_dst = nodes[:, :, FO + 1]
        centred = [sb(f"centred{n}", [P, RB, NODE]) for n in range(2)]
        s_rows = sb("s_rows", [P, N])
        s_now = sb("s_now", [P, ROWS])
        s_turned = sb("s_turned", [JB, P])
        steep_d = sb("steep_d", [P, JB])
        edge = sb("edge", [P, 2])
        edge_all = sb("edge_all", [P, 2])
        d_shift = sb("d_shift", [P, JB])
        s_top = sb("s_top", [P, JB])
        s_guard = sb("s_guard", [P, JB])
        row_args = sb("row_args", [P, 2, JB])
        row_scale = sb("row_scale", [P, 2, JB])
        col_scale = sb("col_scale", [P, 2, JB])
        mean_row = sb("mean_row", [P, F])
        vals = [sb(f"vals{k}", [P, JB, W3], BF16) for k in range(2)]
        cut = [[sb(f"cut{k}_{n}", [P, CUT_MAX, FO]) for n in range(2)] for k in range(2)]

        masks = [sb(f"masks{k}", [P, RB, CCOLS], BF16) for k in range(RING)]
        above = [sb(f"above{k}", [P, UNIT, ROWS], BF16) for k in range(2)]
        pos = [sb(f"pos{k}", [P, UNIT, ROWS], BF16) for k in range(2)]
        neg = [sb(f"neg{k}", [P, UNIT, ROWS], BF16) for k in range(2)]

        sums = sb("sums", [W3, 2, ROWS])
        scaled = [sb(f"scaled{k}", [P, RB, FO]) for k in range(2)]
        total = sb("total", [P, RB, FO])
        lonely = sb("lonely", [P, RB])
        lonely_mean = sb("lonely_mean", [P, RB, F])
        denom = sb("denom", [P, RB])
        inv_denom = sb("inv_denom", [P, RB])
        numer = sb("numer", [P, RB, F])
        att = sb("att", [P, RB, F])
        att_t = sb("att_t", [F, ROWS])
        x_in = [sb(f"x_in{k}", [P, RB, DIM]) for k in range(2)]
        x_fcb = x_in[1]
        x_mid = sb("x_mid", [P, RB, DIM])
        x_fc2b = sb("x_fc2b", [P, RB, DIM])
        h_n = sb("h_n", [P, RB, DIM])
        h_t = sb("h_t", [P, KC, ROWS])
        act_t = sb("act_t", [P, HC, ROWS])
        y_out = sb("y_out", [P, RB, DIM])
        stats = [sb(f"stats{k}", [P, RB, 6]) for k in range(2)]
        mean_var = [sb(f"mean_var{k}", [P, RB, 2]) for k in range(2)]
        var_eps = sb("var_eps", [P, RB])
        mean_rstd = sb("mean_rstd", [P, RB])
        shift = sb("shift", [P, RB])
        rstd = [sb(f"rstd{k}", [P, RB]) for k in range(2)]

        flipped = [pb(f"flipped{k}", [P, UNIT, ROWS], BF16) for k in range(2)]
        acc = [pb(f"acc{k}", [P, ROWS]) for k in range(2)]
        tail = [pb(f"tail{k}", [P, ROWS]) for k in range(2)]

        pre_x = [x_in[0], x_in[1], x_mid, x_fc2b]
        pre_t = [h_t[:], act_t[:, 0:KC, :], act_t[:, KC:2 * KC, :],
                 y_out[:].rearrange("p r d -> p (r d)").rearrange("p (c n) -> p c n", c=KC)]
        DENSE_COLS = 2 * ROWS
        DENSE_STEPS = N // DENSE_COLS
        HALF = N // 2
        dense_adj = [masks[k][:].rearrange("p r c -> p (r c)") for k in range(2)]
        scores = pos[0][:].rearrange("p j r -> p (j r)").bitcast(F32)
        ceiling = neg[0][:].rearrange("p j r -> p (j r)").bitcast(F32)
        weights_t = above[0][:].rearrange("p j r -> p (j r)").bitcast(F32)
        d_rows = s_rows
        dense_s = sb("dense_s", [P, 1])
        dense_tops = sb("dense_tops", [P, DENSE_STEPS])
        dense_top = sb("dense_top", [P, 1])
        s_dram = nc.dram_tensor("s_dram", [1, N], F32).ap()

        w_landed = sem("w_landed")
        gb_landed = sem("gb_landed")
        tail_w_landed = sem("tail_w_landed")
        x_t_landed = [sem(f"x_t_landed{k}") for k in range(X_RING)]
        x_landed = [sem(f"x_landed{k}") for k in range(X_RING)]
        consts = sem("consts")
        wa_ready = sem("wa_ready")
        wa_saved = sem("wa_saved")
        stat_step = sem("stat_step")
        stats_done = sem("stats_done")
        rstd_step = sem("rstd_step")
        rstd_done = sem("rstd_done")
        w_scaled = sem("w_scaled")
        rows_made = sem("rows_made")
        rows_saved = sem("rows_saved")
        node_parts = sem("node_parts")
        projected = sem("projected")
        nodes_saved = sem("nodes_saved")
        s_flipped = sem("s_flipped")
        s_turned_ready = sem("s_turned_ready")
        s_written = sem("s_written")
        s_landed = sem("s_landed")
        node_step = sem("node_step")
        edges_local = sem("edges_local")
        edges_done = sem("edges_done")
        scales_ready = sem("scales_ready")
        mean_ready = sem("mean_ready")
        mean_saved = sem("mean_saved")
        cut_step = [sem(f"cut_step{k}") for k in range(2)]
        vals_ready = [sem(f"vals_ready{k}") for k in range(2)]
        cols_scaled = sem("cols_scaled")
        s_spread = sem("s_spread")

        adj_landed = [sem(f"adj_landed{k}") for k in range(RING)]
        mask_ready = sem("mask_ready")
        unit_flipped = sem("unit_flipped")
        rows_taken = sem("rows_taken")
        above_ready = sem("above_ready")
        pos_ready = sem("pos_ready")
        neg_ready = sem("neg_ready")
        unit_added = sem("unit_added")
        pos_added = sem("pos_added")
        sums_saved = sem("sums_saved")
        folded = sem("folded")
        att_step = sem("att_step")
        att_flipped = sem("att_flipped")
        att_t_ready = sem("att_t_ready")
        proj_ready = sem("proj_ready")
        x_fcb_ready = sem("x_fcb_ready")
        x_mid_ready = sem("x_mid_ready")
        stats2_step = sem("stats2_step")
        stats2_done = sem("stats2_done")
        rstd2_step = sem("rstd2_step")
        rstd2_done = sem("rstd2_done")
        x_fc2b_ready = sem("x_fc2b_ready")
        normed2 = sem("normed2")
        shift_step = sem("shift_step")
        shift_ready = sem("shift_ready")
        h2_flipped = sem("h2_flipped")
        h2_t_done = sem("h2_t_done")
        fc1_ready = sem("fc1_ready")
        gelu_done = sem("gelu_done")
        fc2_ready = sem("fc2_ready")
        y_ready = sem("y_ready")
        y_stored = sem("y_stored")
        x2_landed = sem("x2_landed")
        wide_ready = sem("wide_ready")
        d_flipped = sem("d_flipped")
        d_turned_ready = sem("d_turned_ready")
        d_written = sem("d_written")
        d_landed = sem("d_landed")
        dense_landed = sem("dense_landed")
        dense_step = sem("dense_step")
        dense_scores = sem("dense_scores")
        dense_exps = sem("dense_exps")
        dense_flipped = sem("dense_flipped")
        dense_copied = sem("dense_copied")
        dense_added = sem("dense_added")

        def over_groups(eng, body):
            body(0, first=True)
            with eng.Fori(1, GROUPS - 1) as g:
                body(g)
            body(GROUPS - 1, last=True)

        def over_turns(eng, body):
            body(0, first=True)
            with eng.Fori(1, GROUPS // X_RING - 1) as i:
                body(i)
            body(GROUPS // X_RING - 1, last=True)

        def if_wide(eng):
            eng.wait_ge(wide_ready, 1)
            return eng.If(eng.value_load(wide[0:1, 0:1].bitcast(mybir.dt.int32)) != 0)

        def cut_values(eng, k, b):
            at = slice(*CUTS[b])
            size = at.stop - at.start
            value, rest = cut[k][0][:, 0:size, :], cut[k][1][:, 0:size, :]
            hi, mid, lo = (vals[k][:, at, n * FO:(n + 1) * FO] for n in range(PARTS))
            done = [b * (PARTS + 1)]

            def step(ins):
                done[0] += 1
                ins.then_inc(cut_step[k], 1)
                eng.wait_ge(cut_step[k], done[0])

            step(eng.tensor_tensor(value, wh[:, at, :],
                                   col_scale[:, k, at].unsqueeze(2).to_broadcast([P, size, FO]), ALU.mult))
            step(eng.tensor_copy(hi, value))
            step(eng.tensor_tensor(rest, value, hi, ALU.subtract))
            step(eng.tensor_copy(mid, rest))
            eng.tensor_tensor(lo, rest, mid, ALU.subtract).then_inc(vals_ready[k], 1)
            eng.wait_ge(vals_ready[k], b + 1)

        block = ctx.enter_context(nc.Block())

        @block.sync
        def _(sp):
            def load_x(to, n):
                return sp.dma_start(to[:], x_v[:, bass.ds(n * RB, RB), :])

            def load_x_t(to, n):
                return sp.dma_start(to, x_t_v[:, :, bass.ds(n * ROWS, ROWS)])

            load_x(pre_x[0], 0).then_inc(x_landed[0], 16)
            sp.dma_start(w_tr[:], w_t).then_inc(w_landed, 16)
            sp.dma_start(a_sd[:], a_pair).then_inc(w_landed, 16)
            sp.dma_start(ln1[:], ln1_gb).then_inc(gb_landed, 16)
            sp.dma_start(w_aug[:, :, 0:F], w.rearrange("(c p) f -> p c f", p=P)).then_inc(w_landed, 16)
            for k in range(X_RING):
                load_x_t(pre_t[k], k).then_inc(x_t_landed[k], 16)
                if k > 0:
                    load_x(pre_x[k], k).then_inc(x_landed[k], 16)
            sp.dma_start(ln2[:], ln2_gb).then_inc(tail_w_landed, 16)
            sp.dma_start(fc1b[:], fc1_b).then_inc(tail_w_landed, 16)
            sp.dma_start(fc_sb[:], fc_t).then_inc(tail_w_landed, 16)
            sp.dma_start(fc1_sb[:], fc1_t.rearrange("(c p) h -> p c h", p=P)).then_inc(tail_w_landed, 16)
            sp.dma_start(fc2_sb[:], fc2_t.rearrange("(c p) d -> p c d", p=P)).then_inc(tail_w_landed, 16)
            sp.dma_start(fcb_row[:], fc_b.to_broadcast([P, DIM])).then_inc(tail_w_landed, 16)
            sp.dma_start(fc2b_row[:], fc2_b.to_broadcast([P, DIM])).then_inc(tail_w_landed, 16)

            with sp.Fori(1, GROUPS // X_RING) as i:
                for k in range(X_RING):
                    sp.wait_ge(stat_step, (i - 1) * X_RING + k + 1)
                    load_x(pre_x[k], i * X_RING + k).then_inc(x_landed[k], 16)
                    sp.wait_ge(projected, (i - 1) * X_RING + k + 1)
                    load_x_t(pre_t[k], i * X_RING + k).then_inc(x_t_landed[k], 16)

            def store(q, part, at):
                half = RB // 2
                sp.wait_ge(y_ready, q * 2 + part + 1)
                sp.dma_start(out_v[:, bass.ds(at * RB + part * half, half), :],
                             y_out[:, part * half:(part + 1) * half, :]).then_inc(y_stored, 16)

            def finish(q, at, first=False):
                if not first:
                    sp.wait_ge(x_fcb_ready, q)
                    sp.wait_ge(y_stored, q * 2 * 16)
                load_x(x_in[0], at).then_inc(x2_landed, 16)
                store(q, 0, at)
                store(q, 1, at)

            sp.wait_ge(s_turned_ready, 1)
            sp.dma_start(s_dram.rearrange("a (b p) -> (a b) p", p=P), s_turned[:]).then_inc(s_written, 16)
            sp.wait_ge(s_written, 16)
            sp.dma_start(s_rows[:], s_dram.to_broadcast([P, N])).then_inc(s_landed, 16)

            finish(0, 0, first=True)
            with sp.Fori(1, GROUPS) as q:
                finish(q, q)
            sp.wait_ge(y_stored, 16 * 2 * GROUPS)

            with if_wide(sp):
                sp.wait_ge(d_turned_ready, 1)
                sp.dma_start(s_dram.rearrange("a (b p) -> (a b) p", p=P), s_turned[:]).then_inc(d_written, 16)
                sp.wait_ge(d_written, 16)
                sp.wait_ge(rows_taken, GROUPS)
                sp.dma_start(d_rows[:], s_dram.to_broadcast([P, N])).then_inc(d_landed, 16)
                with sp.Fori(0, GROUPS) as g:
                    finish(GROUPS + g, g)
                sp.wait_ge(y_stored, 16 * 4 * GROUPS)

        @block.gpsimd
        def _(pool):
            def load_chunk(g, c):
                pool.dma_start(masks[c % RING][:], adj_v[:, bass.ds(g * RB, RB), c * CCOLS:(c + 1) * CCOLS])\
                    .then_inc(adj_landed[c % RING], 16)

            nc.gpsimd.memset(ident[:], 0.0).then_inc(consts, 1)
            nc.gpsimd.memset(fold3[:], 0.0).then_inc(consts, 1)
            nc.gpsimd.memset(minus_half[:], -0.5).then_inc(consts, 1)
            nc.gpsimd.memset(eps[:], EPS).then_inc(consts, 1)
            nc.gpsimd.memset(w_aug[:, :, F:FO], 0.0).then_inc(consts, 1)
            nc.gpsimd.memset(b_row[:, F:FO], 1.0).then_inc(consts, 1)
            nc.gpsimd.memset(minus_ones[:], -1.0).then_inc(consts, 1)
            nc.gpsimd.memset(ones_n[:], 1.0 / N).then_inc(consts, 1)
            pool.wait_ge(consts, CONSTS)
            nc.gpsimd.affine_select(out=ident[:], in_=ident[:], compare_op=ALU.not_equal, fill=1.0,
                                    base=0, pattern=[[-1, P]], channel_multiplier=1).then_inc(consts, 1)
            for part in range(PARTS):
                nc.gpsimd.affine_select(out=fold3[:], in_=fold3[:], compare_op=ALU.not_equal, fill=1.0,
                                        base=-part * FO, pattern=[[-1, FO]], channel_multiplier=1)\
                    .then_inc(consts, 1)
                pool.wait_ge(consts, CONSTS + 2 + part)
            nc.gpsimd.tensor_copy(identb[:], ident[:]).then_inc(consts, 1)

            def inverse_deviation(step, base, mv, to, done):
                nc.gpsimd.tensor_tensor(var_eps[:], mv[:, :, 1], eps[:], ALU.add).then_inc(step, 1)
                pool.wait_ge(step, base + 1)
                nc.gpsimd.tensor_tensor(to[:], var_eps[:], minus_half[:], ALU.pow).then_inc(done, 1)
                pool.wait_ge(done, base + 1)

            def turn(i):
                for k in range(X_RING):
                    t = i * X_RING + k
                    pool.wait_ge(stats_done, t + 1)
                    inverse_deviation(rstd_step, t, mean_var[k % 2], rstd[k % 2], rstd_done)

            with pool.Fori(0, GROUPS // X_RING - 1) as i:
                turn(i)
            for c in range(AHEAD):
                load_chunk(0, c)
            turn(GROUPS // X_RING - 1)

            pool.wait_ge(edges_local, 2)
            nc.gpsimd.partition_all_reduce(edge_all[:], edge[:], P, RMAX).then_inc(edges_done, 1)

            pool.wait_ge(cols_scaled, 1)
            cut_values(pool, 1, 0)
            pool.wait_ge(tail_w_landed, 7 * 16)

            def body(g, first=False, last=False):
                q = g - 1
                for c in range(CHUNKS):
                    if not (last and c + AHEAD >= CHUNKS):
                        if not (first and c == 0):
                            pool.wait_ge(unit_flipped, g * UNITS + 2 * c)
                        ahead = c + AHEAD
                        load_chunk(g + ahead // CHUNKS, ahead % CHUNKS)
                    if first:
                        for k, b in CUT_AT_CHUNK.get(c, ()):
                            if k == 0:
                                pool.wait_ge(vals_ready[0], b)
                            cut_values(pool, k, b)
                    if not first:
                        finish_rows(q, c)

            def finish_rows(q, c):
                if c == 0:
                    pool.wait_ge(x2_landed, 16 * (q + 1))
                    nc.gpsimd.tensor_tensor(x_fcb[:], x_in[0][:],
                                            fcb_row[:].unsqueeze(1).to_broadcast([P, RB, DIM]),
                                            ALU.add).then_inc(x_fcb_ready, 1)
                if c == 2:
                    pool.wait_ge(stats2_done, q + 1)
                    inverse_deviation(rstd2_step, q, mean_var[0], rstd[0], rstd2_done)
                    nc.gpsimd.tensor_tensor(mean_rstd[:], mean_var[0][:, :, 0], rstd[0][:], ALU.mult)\
                        .then_inc(shift_step, 1)
                    pool.wait_ge(shift_step, q + 1)
                    nc.gpsimd.tensor_tensor(shift[:], mean_rstd[:], minus_ones[:, 0:RB], ALU.mult)\
                        .then_inc(shift_ready, 1)
                    pool.wait_ge(x_mid_ready, q + 1)
                    nc.gpsimd.tensor_tensor(x_fc2b[:], x_mid[:],
                                            fc2b_row[:].unsqueeze(1).to_broadcast([P, RB, DIM]),
                                            ALU.add).then_inc(x_fc2b_ready, 1)

            over_groups(pool, body)
            for c in range(CHUNKS):
                finish_rows(GROUPS - 1, c)

            with if_wide(pool):
                pool.wait_ge(unit_flipped, GROUPS * UNITS)
                with pool.Fori(0, GROUPS) as g:
                    with pool.Fori(0, RB) as r:
                        n = g * RB + r
                        pool.wait_ge(att_step, GROUPS * ATT_STEPS + g * ATT_STEPS + r * DENSE_ATT_STEP)
                        for k in range(2):
                            pool.dma_start(dense_adj[k], adj_v[:, n, k * HALF:(k + 1) * HALF])\
                                .then_inc(dense_landed, 16)
                    for c in range(CHUNKS):
                        finish_rows(GROUPS + g, c)

        def affine_flip(to, got, gb, ready):
            for c in range(KC):
                last = nc.scalar.activation(to[:, c, :], got[c], ACT.Identity,
                                            bias=gb[:, 1, c:c + 1], scale=gb[:, 0, c:c + 1])
            last.then_inc(ready, 1)

        @block.scalar
        def _(act):
            act.wait_ge(wa_ready, 1)
            for c in range(KC):
                last = nc.scalar.activation(w_aug[:, c, FO:NODE], acc[1][:, 2 * c:2 * c + 2], ACT.Copy)
            last.then_inc(wa_saved, 1)
            act.wait_ge(wa_saved, 1)
            act.wait_ge(w_landed, 3 * 16)
            act.wait_ge(gb_landed, 16)
            act.wait_ge(consts, CONSTS)
            for c in range(KC):
                last = nc.scalar.activation(w_g[:, c, :], w_aug[:, c, :], ACT.Identity, scale=ln1[:, 0, c:c + 1])
            last.then_inc(w_scaled, 1)
            act.wait_ge(rows_made, 1)
            nc.scalar.activation(c_row[:], tail[0][:, 0:NODE], ACT.Copy)
            nc.scalar.activation(b_row[:, 0:F], tail[1][:, 0:F], ACT.Copy)
            nc.scalar.activation(b_row[:, FO:NODE], tail[1][:, FO:NODE], ACT.Copy).then_inc(rows_saved, 1)

            act.wait_ge(s_flipped, 1)
            nc.scalar.activation(s_turned[:], tail[1][0:JB, 0:P], ACT.Copy).then_inc(s_turned_ready, 1)

            act.wait_ge(node_step, 2)
            nc.scalar.activation(col_scale[:, 0, :], d_shift[:], ACT.Exp)
            nc.scalar.activation(col_scale[:, 1, :], d_shift[:], ACT.Exp, scale=ALPHA).then_inc(cols_scaled, 1)

            def mark(g, u):
                for j in range(UNIT):
                    jb = u * UNIT + j
                    last = nc.scalar.activation(above[u % 2][:, j, :], s_now[:],
                                                ACT.Relu, bias=steep_d[:, jb:jb + 1])
                last.then_inc(above_ready, 1)

            def finish_rows(q, u):
                if u == 0:
                    act.wait_ge(pos_added, q + 1)
                    nc.scalar.activation(sums[:, 0, :], acc[0][0:W3, :], ACT.Copy)
                    act.wait_ge(unit_added, (q + 1) * UNITS)
                    nc.scalar.activation(sums[:, 1, :], acc[1][0:W3, :], ACT.Copy).then_inc(sums_saved, 1)
                if u == 3:
                    act.wait_ge(att_flipped, q + 1)
                    nc.scalar.activation(att_t[:], tail[1][0:F, :], ACT.Copy).then_inc(att_t_ready, 1)
                if u == NORM_AT:
                    act.wait_ge(x_mid_ready, q + 1)
                    act.wait_ge(shift_ready, q + 1)
                    for r in range(RB):
                        last = nc.scalar.activation(h_n[:, r, :], x_mid[:, r, :], ACT.Identity,
                                                    bias=shift[:, r:r + 1], scale=rstd[0][:, r:r + 1])
                    last.then_inc(normed2, 1)
                if u == 7:
                    act.wait_ge(h2_flipped, q + 1)
                    affine_flip(h_t, [t[:] for t in tail], ln2, h2_t_done)
                if 8 <= u < 8 + HC:
                    m = u - 8
                    act.wait_ge(fc1_ready, q * HC + m + 1)
                    nc.scalar.activation(act_t[:, m, :], tail[m % 2][:], ACT.Gelu,
                                         bias=fc1b[:, m:m + 1]).then_inc(gelu_done, 1)

            def body(g, first=False, last=False):
                for u in range(UNITS):
                    if not (last and u == UNITS - 1):
                        if u == UNITS - 1:
                            act.wait_ge(rows_taken, g + 2)
                        if not (first and u == 0):
                            act.wait_ge(pos_ready, g * UNITS + u)
                        nxt = u + 1
                        mark(g + nxt // UNITS, nxt % UNITS)
                    if not first:
                        finish_rows(g - 1, u)

            act.wait_ge(tail_w_landed, 7 * 16)
            act.wait_ge(rows_taken, 1)
            mark(0, 0)
            act.wait_ge(node_step, NODE_STEPS)
            nc.scalar.activation(row_scale[:], row_args[:], ACT.Exp).then_inc(scales_ready, 1)
            nc.scalar.preload_act_table(ACT.Gelu)
            over_groups(act, body)
            for u in range(UNITS):
                finish_rows(GROUPS - 1, u)

            with if_wide(act):
                act.wait_ge(s_written, 16)
                act.wait_ge(d_flipped, 1)
                nc.scalar.activation(s_turned[:], tail[1][0:JB, 0:P], ACT.Copy).then_inc(d_turned_ready, 1)
                with act.Fori(0, GROUPS) as g:
                    with act.Fori(0, RB) as r:
                        with act.Fori(0, DENSE_STEPS) as c:
                            K = (g * RB + r) * DENSE_STEPS + c
                            act.wait_ge(dense_scores, K + 1)
                            nc.scalar.activation(scores, scores, ACT.Exp, bias=dense_top[:])\
                                .then_inc(dense_exps, 1)
                            act.wait_ge(dense_flipped, K + 1)
                            for k in range(2):
                                last = nc.scalar.activation(weights_t[:, k * ROWS:(k + 1) * ROWS],
                                                            tail[k][:], ACT.Copy)
                            last.then_inc(dense_copied, 1)
                    for u in range(1, UNITS):
                        finish_rows(GROUPS + g, u)

        @block.tensor
        def _(pe):
            pe.wait_ge(w_landed, 3 * 16)
            for c in range(KC):
                last = nc.tensor.matmul(acc[1][:, 2 * c:2 * c + 2], w_tr[:, c * P:(c + 1) * P], a_sd[:],
                                        start=True, stop=True)
            last.then_inc(wa_ready, 1)

            def flip_rows(rows, to, done):
                for c in range(KC):
                    for r in range(RB):
                        last = nc.tensor.transpose(to[c][:, r * P:(r + 1) * P],
                                                   rows[:, r, c * P:(c + 1) * P], ident[:])
                last.then_inc(done, 1)

            def project(i, k, free=True):
                t = i * X_RING + k
                pe.wait_ge(x_t_landed[k], i * 16 + 16)
                if free:
                    pe.wait_ge(nodes_saved, t - 1)
                for r in range(RB):
                    for c in range(KC):
                        last = nc.tensor.matmul(acc[k % 2][:, r * NODE:(r + 1) * NODE],
                                                pre_t[k][:, c, r * P:(r + 1) * P], w_g[:, c, :],
                                                start=(c == 0), stop=(c == KC - 1))
                last.then_inc(projected, 1)

            pe.wait_ge(w_scaled, 1)
            for c in range(KC):
                nc.tensor.matmul(tail[0][:, 0:NODE], minus_ones[:], w_g[:, c, :],
                                 start=(c == 0), stop=(c == KC - 1))
            for c in range(KC):
                last = nc.tensor.matmul(tail[1][:, 0:NODE], ln1[:, 1, c:c + 1].to_broadcast([P, P]),
                                        w_aug[:, c, :], start=(c == 0), stop=(c == KC - 1))
            last.then_inc(rows_made, 1)
            for k in range(X_RING):
                project(0, k, free=k >= 2)
            with pe.Fori(1, GROUPS // X_RING) as i:
                for k in range(X_RING):
                    project(i, k)

            pe.wait_ge(consts, CONSTS_ALL)
            pe.wait_ge(nodes_saved, GROUPS)
            nc.tensor.transpose(tail[1][0:JB, 0:P], f_src, ident[:]).then_inc(s_flipped, 1)
            for r in range(RB):
                last = nc.tensor.matmul(tail[0][:, r * P:(r + 1) * P], nodes[:, r, FO:FO + 1].to_broadcast([P, P]),
                                        ident[:], start=True, stop=True)
            last.then_inc(s_spread, 1)

            def flip(g, u):
                c = u // 2
                if u % 2 == 0:
                    pe.wait_ge(mask_ready, g * CHUNKS + c + 1)
                for j in range(UNIT):
                    col = (u % 2 * UNIT + j) * P
                    for r in range(RB):
                        last = nc.tensor.transpose(flipped[u % 2][:, j, r * P:(r + 1) * P],
                                                   masks[c % RING][:, r, col:col + P], identb[:])
                last.then_inc(unit_flipped, 1)

            def add(g, u):
                for k, side, ready in ((0, pos, pos_ready), (1, neg, neg_ready)):
                    pe.wait_ge(ready, g * UNITS + u + 1)
                    for j in range(UNIT):
                        jb = u * UNIT + j
                        last = nc.tensor.matmul(acc[k][0:W3, :], vals[k][:, jb, :], side[u % 2][:, j, :],
                                                start=(jb == 0), stop=(jb == JB - 1))
                    if k == 0 and u == UNITS - 1:
                        last.then_inc(pos_added, 1)
                last.then_inc(unit_added, 1)

            def finish_rows(q, u):
                if u == 1:
                    pe.wait_ge(sums_saved, q + 1)
                    for r in range(RB):
                        for k in range(2):
                            last = nc.tensor.matmul(tail[0][:, (2 * r + k) * FO:(2 * r + k + 1) * FO],
                                                    sums[:, k, r * P:(r + 1) * P], fold3[:],
                                                    start=True, stop=True)
                    last.then_inc(folded, 1)
                if u == 3:
                    pe.wait_ge(att_step, (q + 1) * ATT_STEPS)
                    for r in range(RB):
                        last = nc.tensor.transpose(tail[1][0:F, r * P:(r + 1) * P], att[:, r, :], ident[:])
                    last.then_inc(att_flipped, 1)
                if u == 4:
                    pe.wait_ge(att_t_ready, q + 1)
                    for r in range(RB):
                        last = nc.tensor.matmul(tail[r // 2][:, r % 2 * DIM:(r % 2 + 1) * DIM],
                                                att_t[:, r * P:(r + 1) * P], fc_sb[:], start=True, stop=True)
                    last.then_inc(proj_ready, 1)
                if u == 7:
                    pe.wait_ge(normed2, q + 1)
                    flip_rows(h_n, tail, h2_flipped)
                if 8 <= u < 8 + HC:
                    m = u - 8
                    pe.wait_ge(h2_t_done, q + 1)
                    if m >= 2:
                        pe.wait_ge(gelu_done, q * HC + m - 1)
                    for c in range(KC):
                        last = nc.tensor.matmul(tail[m % 2][:], fc1_sb[:, c, m * P:(m + 1) * P], h_t[:, c, :],
                                                start=(c == 0), stop=(c == KC - 1))
                    last.then_inc(fc1_ready, 1)
                if 12 <= u < 15:
                    pe.wait_ge(gelu_done, (q + 1) * HC)
                    for r in ((0,), (1,), (2, 3))[u - 12]:
                        for m in range(HC):
                            last = nc.tensor.matmul(tail[r // 2][:, r % 2 * DIM:(r % 2 + 1) * DIM],
                                                    act_t[:, m, r * P:(r + 1) * P], fc2_sb[:, m, :],
                                                    start=(m == 0), stop=(m == HC - 1))
                    if u > 12:
                        last.then_inc(fc2_ready, 1)

            def body(g, first=False, last=False):
                for u in range(UNITS):
                    if not (first and u < 2):
                        pe.wait_ge(neg_ready, g * UNITS + u - 1)
                    flip(g, u)
                    if not first and u in FINISH_FIRST:
                        finish_rows(g - 1, u)
                    if u > 0:
                        if u == 1 and not first:
                            pe.wait_ge(sums_saved, g)
                        for b, (start, _) in enumerate(CUTS):
                            if first and start == (u - 1) * UNIT:
                                for k in range(2):
                                    pe.wait_ge(vals_ready[k], b + 1)
                        add(g, u - 1)
                    elif not first:
                        add(g - 1, UNITS - 1)
                    if not first and u not in FINISH_FIRST:
                        finish_rows(g - 1, u)
                    if first and u < MEAN_PIECES:
                        if u == 0:
                            pe.wait_ge(s_turned_ready, 1)
                        at = slice(u * JB // MEAN_PIECES, (u + 1) * JB // MEAN_PIECES)
                        sums_up = nc.tensor.matmul(tail[1][:].rearrange("p (n f) -> p n f", f=F), ones_n[:],
                                                   nodes[:, at, 0:F], start=(u == 0),
                                                   stop=(u == MEAN_PIECES - 1))
                        if u == MEAN_PIECES - 1:
                            sums_up.then_inc(mean_ready, 1)
                    if first and u == UNITS - 1:
                        pe.wait_ge(mean_saved, 1)

            over_groups(pe, body)
            add(GROUPS - 1, UNITS - 1)
            pe.wait_ge(tail_w_landed, 7 * 16)
            for u in range(UNITS):
                finish_rows(GROUPS - 1, u)

            with if_wide(pe):
                pe.wait_ge(y_ready, 2 * GROUPS)
                nc.tensor.transpose(tail[1][0:JB, 0:P], f_dst, ident[:]).then_inc(d_flipped, 1)
                with pe.Fori(0, GROUPS) as g:
                    with pe.Fori(0, RB) as r:
                        for c in range(DENSE_STEPS):
                            K = (g * RB + r) * DENSE_STEPS + c
                            blocks = DENSE_COLS // P
                            pe.wait_ge(dense_exps, K + 1)
                            for b in range(blocks):
                                last = nc.tensor.transpose(tail[b // RB][:, b % RB * P:(b % RB + 1) * P],
                                                           scores[:, b * P:(b + 1) * P], ident[:])
                            last.then_inc(dense_flipped, 1)
                            pe.wait_ge(dense_copied, K + 1)
                            for b in range(blocks):
                                jb = c * blocks + b
                                last = nc.tensor.matmul(acc[0][:, 0:FO], weights_t[:, b * P:(b + 1) * P],
                                                        wh[:, jb, :], start=(jb == 0), stop=(jb == JB - 1))
                            last.then_inc(dense_added, 1)
                    for u in range(2, UNITS):
                        finish_rows(GROUPS + g, u)

        @block.vector
        def _(dve):
            def row_stats(xt, st, mv, step, base, done):
                for r in range(RB):
                    last = nc.vector.bn_stats(st[:, r, :], xt[:, r, :])
                last.then_inc(step, 1)
                dve.wait_ge(step, base + 1)
                nc.vector.memset(scratch[:], 0.0)
                for r in range(RB):
                    last = nc.vector.bn_aggr(mv[:, r, :], st[:, r, :])
                last.then_inc(done, 1)

            def stats_of(i, k):
                dve.wait_ge(x_landed[k], i * 16 + 16)
                row_stats(pre_x[k], stats[k % 2], mean_var[k % 2], stat_step, i * X_RING + k, stats_done)

            def make_nodes(t, k):
                dve.wait_ge(projected, t + 1)
                for r in range(RB):
                    last = nc.vector.scalar_tensor_tensor(out=centred[0][:, r, :], in0=c_row[:],
                                                          scalar=mean_var[k][:, r, 0:1],
                                                          in1=acc[k][:, r * NODE:(r + 1) * NODE],
                                                          op0=ALU.mult, op1=ALU.add)
                last.then_inc(node_parts, 1)
                dve.wait_ge(node_parts, 2 * t + 1)
                dve.wait_ge(rstd_done, t + 1)
                nc.vector.tensor_tensor(centred[1][:], centred[0][:],
                                        rstd[k][:].unsqueeze(2).to_broadcast([P, RB, NODE]), ALU.mult)\
                    .then_inc(node_parts, 1)
                dve.wait_ge(node_parts, 2 * t + 2)
                nc.vector.tensor_tensor(nodes[:, bass.ds(t * RB, RB), :], centred[1][:],
                                        b_row[:].unsqueeze(1).to_broadcast([P, RB, NODE]), ALU.add)\
                    .then_inc(nodes_saved, 1)

            def turn(i, first=False, last=False):
                for k in range(X_RING):
                    if not (last and k == X_RING - 1):
                        stats_of(i + (k + 1) // X_RING, (k + 1) % X_RING)
                    if first and k == 0:
                        dve.wait_ge(rows_saved, 1)
                    make_nodes(i * X_RING + k, k % 2)

            stats_of(0, 0)
            over_turns(dve, turn)

            steps = [0]

            def node(ins):
                steps[0] += 1
                ins.then_inc(node_step, 1)
                dve.wait_ge(node_step, steps[0])

            def clean(g, c):
                dve.wait_ge(adj_landed[c % RING], (g * (CHUNKS // RING) + c // RING + 1) * 16)
                m = masks[c % RING]
                nc.vector.tensor_scalar(m[:], m[:], 0.0, 1.0, ALU.max, ALU.min).then_inc(mask_ready, 1)

            clean(0, 0)
            dve.wait_ge(nodes_saved, GROUPS)
            nc.vector.reduce_max(edge[:, 0:1], f_dst, AX_X).then_inc(edges_local, 1)
            nc.vector.tensor_reduce(edge[:, 1:2], f_dst, AX_X, ALU.min, negate=True)\
                .then_inc(edges_local, 1)
            node(nc.vector.tensor_scalar(steep_d[:], f_dst, STEEP, None, ALU.mult))
            dve.wait_ge(edges_done, 1)
            node(nc.vector.tensor_scalar(d_shift[:], f_dst, edge_all[:, 0:1], None, ALU.subtract))

            def take_rows(g):
                nc.vector.tensor_scalar(s_now[:], s_rows[:, bass.ds(g * ROWS, ROWS)], STEEP, None, ALU.mult)\
                    .then_inc(rows_taken, 1)

            def finish_rows(q, u):
                if u == 2:
                    dve.wait_ge(folded, q + 1)
                    got = tail[0][:, 0:RB * 2 * FO].rearrange("p (r k f) -> p r k f", r=RB, k=2)
                    n = [0]

                    def step(ins):
                        n[0] += 1
                        ins.then_inc(att_step, 1)
                        if n[0] < ATT_STEPS:
                            dve.wait_ge(att_step, q * ATT_STEPS + n[0])

                    for k in range(2):
                        last = nc.vector.tensor_tensor(
                            scaled[k][:], got[:, :, k, :],
                            row_scale[:, k, bass.ds(q * RB, RB)].unsqueeze(2).to_broadcast([P, RB, FO]),
                            ALU.mult)
                    step(last)
                    step(nc.vector.tensor_tensor(total[:], scaled[0][:], scaled[1][:], ALU.add))
                    step(nc.vector.tensor_scalar(lonely[:], total[:, :, F], 0.0, None, ALU.is_equal))
                    nc.vector.tensor_tensor(lonely_mean[:], lonely[:].unsqueeze(2).to_broadcast([P, RB, F]),
                                            mean_row[:].unsqueeze(1).to_broadcast([P, RB, F]), ALU.mult)
                    step(nc.vector.scalar_tensor_tensor(out=denom[:], in0=total[:, :, F], scalar=TINY,
                                                        in1=lonely[:], op0=ALU.max, op1=ALU.add))
                    nc.vector.tensor_tensor(numer[:], total[:, :, 0:F], lonely_mean[:], ALU.add)
                    step(nc.vector.reciprocal(inv_denom[:], denom[:]))
                    step(nc.vector.tensor_tensor(att[:], numer[:],
                                                 inv_denom[:].unsqueeze(2).to_broadcast([P, RB, F]), ALU.mult))
                    assert n[0] == ATT_STEPS
                if u == 5:
                    dve.wait_ge(proj_ready, q + 1)
                    dve.wait_ge(x_fcb_ready, q + 1)
                    for k in range(2):
                        rows = slice(k * RB // 2, (k + 1) * RB // 2)
                        last = nc.vector.tensor_tensor(x_mid[:, rows, :],
                                                       tail[k][:].rearrange("p (r d) -> p r d", d=DIM),
                                                       x_fcb[:, rows, :], ALU.add)
                    last.then_inc(x_mid_ready, 1)
                    dve.wait_ge(x_mid_ready, q + 1)
                    row_stats(x_mid, stats[0], mean_var[0], stats2_step, q, stats2_done)
                if u in (14, 15):
                    k = u - 14
                    rows = slice(k * RB // 2, (k + 1) * RB // 2)
                    dve.wait_ge(fc2_ready, q * 2 + k + 1)
                    dve.wait_ge(x_fc2b_ready, q + 1)
                    nc.vector.tensor_tensor(y_out[:, rows, :], tail[k][:].rearrange("p (r d) -> p r d", d=DIM),
                                            x_fc2b[:, rows, :], ALU.add).then_inc(y_ready, 1)

            def body(g, first=False, last=False):
                for u in range(UNITS):
                    if u in CLEAN_AT and not (last and CLEAN_AT[u] == CHUNKS) and not (first and u == 0):
                        c = CLEAN_AT[u]
                        clean(g + c // CHUNKS, c % CHUNKS)
                    if first and u in CUT_AT_UNIT:
                        cut_values(dve, 0, CUT_AT_UNIT[u])
                    if first and u == MEAN_AT:
                        node(nc.vector.tensor_tensor(f_dst_range[:], edge_all[:, 0:1], edge_all[:, 1:2], ALU.add))
                        nc.vector.tensor_scalar(wide[:], f_dst_range[:], WIDE, None, ALU.is_gt)\
                            .then_inc(wide_ready, 1)
                        dve.wait_ge(mean_ready, 1)
                        nc.vector.reduce_sum(mean_row[:], tail[1][:].rearrange("p (n f) -> p f n", f=F), AX_X)\
                            .then_inc(mean_saved, 1)
                    if first and u == UNITS - 1:
                        dve.wait_ge(s_landed, 16)
                        dve.wait_ge(scales_ready, 1)
                    if u == UNITS - 1 and not last:
                        dve.wait_ge(above_ready, (g + 1) * UNITS)
                        take_rows(g + 1)
                    if not first:
                        finish_rows(g - 1, u)
                    U = g * UNITS + u
                    dve.wait_ge(unit_flipped, U + 1)
                    dve.wait_ge(above_ready, U + 1)
                    if not (first and u < 2):
                        dve.wait_ge(unit_added, U - 1)
                    nc.vector.tensor_tensor(pos[u % 2][:], above[u % 2][:], flipped[u % 2][:], ALU.min)\
                        .then_inc(pos_ready, 1)
                    dve.wait_ge(pos_ready, U + 1)
                    nc.vector.tensor_tensor(neg[u % 2][:], flipped[u % 2][:], pos[u % 2][:], ALU.subtract)\
                        .then_inc(neg_ready, 1)
                    if first and u == 0:
                        clean(0, 1)

            dve.wait_ge(s_spread, 1)
            nc.vector.tensor_scalar(s_now[:], tail[0][:], STEEP, None, ALU.mult).then_inc(rows_taken, 1)
            dve.wait_ge(cols_scaled, 1)
            cut_values(dve, 0, 0)
            node(nc.vector.tensor_scalar(s_top[:], f_src, edge_all[:, 0:1], None, ALU.add))
            node(nc.vector.scalar_tensor_tensor(out=s_guard[:], in0=s_top[:], scalar=ALPHA, in1=s_top[:],
                                                op0=ALU.mult, op1=ALU.max))
            node(nc.vector.tensor_tensor(row_args[:, 0, :], s_top[:], s_guard[:], ALU.subtract))
            node(nc.vector.scalar_tensor_tensor(out=row_args[:, 1, :], in0=s_top[:], scalar=ALPHA,
                                                in1=s_guard[:], op0=ALU.mult, op1=ALU.subtract))
            assert steps[0] == NODE_STEPS
            over_groups(dve, body)
            for u in range(UNITS):
                finish_rows(GROUPS - 1, u)

            def dense_row_block(g, r):
                n = g * RB + r
                PER_BLOCK = 1 + DENSE_STEPS * (5 + 3) + 2
                count = [0]

                def step(ins):
                    count[0] += 1
                    ins.then_inc(dense_step, 1)
                    dve.wait_ge(dense_step, n * PER_BLOCK + count[0])

                def masked_scores(c):
                    half, at = divmod(c * DENSE_COLS, HALF)
                    step(nc.vector.tensor_scalar(scores, d_rows[:, c * DENSE_COLS:(c + 1) * DENSE_COLS],
                                                 dense_s[:], None, ALU.add))
                    step(nc.vector.scalar_tensor_tensor(out=scores, in0=scores, scalar=ALPHA, in1=scores,
                                                        op0=ALU.mult, op1=ALU.max))
                    step(nc.vector.tensor_scalar(ceiling, dense_adj[half][:, at:at + DENSE_COLS],
                                                 -2.0 * MASKED, MASKED, ALU.mult, ALU.add))
                    return nc.vector.tensor_tensor(scores, scores, ceiling, ALU.min)

                dve.wait_ge(dense_landed, (n + 1) * 32)
                nc.vector.tensor_copy(dense_s[:], nodes[:, bass.ds(n, 1), FO])
                for k in range(2):
                    last = nc.vector.tensor_scalar(dense_adj[k], dense_adj[k], 0.0, 1.0, ALU.max, ALU.min)
                step(last)
                for c in range(DENSE_STEPS):
                    step(masked_scores(c))
                    step(nc.vector.reduce_max(dense_tops[:, c:c + 1], scores, AX_X))
                step(nc.vector.tensor_reduce(dense_top[:], dense_tops[:], AX_X, ALU.max, negate=True))
                for c in range(DENSE_STEPS):
                    if c > 0:
                        dve.wait_ge(dense_flipped, n * DENSE_STEPS + c)
                    masked_scores(c).then_inc(dense_scores, 1)
                    dve.wait_ge(dense_scores, n * DENSE_STEPS + c + 1)
                dve.wait_ge(dense_added, (n + 1) * DENSE_STEPS)
                step(nc.vector.reciprocal(inv_denom[:, 0:1], acc[0][:, F:FO]))
                nc.vector.tensor_scalar(att[:, bass.ds(r, 1), :].rearrange("p r f -> p (r f)"),
                                        acc[0][:, 0:F], inv_denom[:, 0:1], None, ALU.mult)\
                    .then_inc(att_step, DENSE_ATT_STEP)
                assert count[0] == PER_BLOCK
                dve.wait_ge(att_step, (GROUPS + g) * ATT_STEPS + (r + 1) * DENSE_ATT_STEP)

            with if_wide(dve):
                dve.wait_ge(d_landed, 16)
                with dve.Fori(0, GROUPS) as g:
                    with dve.Fori(0, RB) as r:
                        dense_row_block(g, r)
                    nc.vector.memset(scratch[:], 0.0).then_inc(att_step, ATT_STEPS - RB * DENSE_ATT_STEP)
                    for u in range(3, UNITS):
                        finish_rows(GROUPS + g, u)


def kernel(x, adj, L0_gnn_W, L0_gnn_a, L0_gnn_fc_w, L0_gnn_fc_b, L0_gnn_ln1_g, L0_gnn_ln1_b,
           L0_gnn_ln2_g, L0_gnn_ln2_b, L0_gnn_fc1_w, L0_gnn_fc1_b, L0_gnn_fc2_w, L0_gnn_fc2_b):
    import numpy as np
    import concourse.bacc as bacc
    from concourse.bass_utils import run_bass_kernel_spmd

    def columns(v):
        return np.asarray(v).reshape(-1, P).T

    laid = {
        "x": np.asarray(x),
        "x_t": np.asarray(x).T,
        "adj": np.asarray(adj),
        "w": np.asarray(L0_gnn_W),
        "w_t": np.asarray(L0_gnn_W).T,
        "a_pair": np.asarray(L0_gnn_a).reshape(2, -1).T,
        "fc_t": np.asarray(L0_gnn_fc_w).T,
        "fc_b": np.asarray(L0_gnn_fc_b)[None, :],
        "ln1_gb": np.stack([columns(L0_gnn_ln1_g), columns(L0_gnn_ln1_b)], axis=1),
        "ln2_gb": np.stack([columns(L0_gnn_ln2_g), columns(L0_gnn_ln2_b)], axis=1),
        "fc1_t": np.asarray(L0_gnn_fc1_w).T,
        "fc1_b": columns(L0_gnn_fc1_b),
        "fc2_t": np.asarray(L0_gnn_fc2_w).T,
        "fc2_b": np.asarray(L0_gnn_fc2_b)[None, :],
    }
    nc = bacc.Bacc("TRN2", target_bir_lowering=False, num_devices=1)
    arrays, args = {}, []
    for name, v in laid.items():
        arrays[f"in_{name}"] = np.ascontiguousarray(v)
        args.append(nc.dram_tensor(f"in_{name}", v.shape, mybir.dt.from_np(v.dtype), kind="ExternalInput").ap())
    out = nc.dram_tensor("out", laid["x"].shape, F32, kind="ExternalOutput").ap()
    build_gat(nc, *args, out)
    r = run_bass_kernel_spmd(nc, [arrays], core_ids=[0])
    return r.results[0]["out"]
```
